# Optimizing a Trainium2 kernel written in Bass

```python
import numpy as np
import jax
import jax.numpy as jnp

def _softmax(x, axis=-1):
    return jax.nn.softmax(x, axis=axis)
def _gelu(x):
    return jax.nn.gelu(x, approximate=True)
def _silu(x):
    return jax.nn.silu(x)
def _sigmoid(x):
    return jax.nn.sigmoid(x)
def _layernorm(x, axis=-1, eps=1e-5):
    m = jnp.mean(x, axis=axis, keepdims=True)
    v = jnp.var(x, axis=axis, keepdims=True)
    return (x - m) / jnp.sqrt(v + eps)
def _scatter_add(tgt, idx, src, axis=0):
    return tgt.at[idx].add(src)
def _segment_sum(src, seg, n):
    return jax.ops.segment_sum(src, seg, n)

kernel_name = 'mk_conv_seq_d1_conv_nchw256_033a64'

def setup_inputs(seed: int = 0):
    np.random.seed(seed)
    _w = jnp.asarray
    def _rec_inputs():
        import jax
        import jax.numpy as jnp
        _gk = jax.random.key(seed)
        x = -0.0002144 + 1 * jax.random.normal(jax.random.fold_in(_gk, 1), (16, 256, 40, 40), jnp.float32)
        return x
    x = _rec_inputs()
    def _L0_conv_setup():
        import jax, jax.numpy as jnp
        import numpy as np
        WR = 14
        KEY_DIM = 16
        D = 64
        NH = 4
        SCALE = KEY_DIM ** (-0.5)
        EPS = 1e-06

        def _bias_idxs(wr):
            pts = [(i, j) for i in range(wr) for j in range(wr)]
            offmap, idxs = ({}, [])
            for p1 in pts:
                for p2 in pts:
                    off = (abs(p1[0] - p2[0]), abs(p1[1] - p2[1]))
                    if off not in offmap:
                        offmap[off] = len(offmap)
                    idxs.append(offmap[off])
            return np.array(idxs, np.int32).reshape(wr * wr, wr * wr)
        BIAS_IDXS = _bias_idxs(WR)

        def _layernorm_cf(x, w, b):
            u = x.mean(1, keepdims=True)
            s = ((x - u) ** 2).mean(1, keepdims=True)
            xn = (x - u) / jnp.sqrt(s + EPS)
            return w[None, :, None, None] * xn + b[None, :, None, None]

        def _conv1x1(x, w, b):
            return jnp.einsum('bchw,oc->bohw', x, w) + b[None, :, None, None]

        def _cascaded_attn(xw, Wqkv, bqkv, Wdw, bdw, Wproj, bproj, attn_bias):
            Bw, C, H, W = xw.shape
            N = H * W
            bias = attn_bias[:, BIAS_IDXS]
            chunks = jnp.split(xw, NH, axis=1)
            feats = []
            feat = chunks[0]
            for i in range(NH):
                if i > 0:
                    feat = feat + chunks[i]
                qkv = _conv1x1(feat, Wqkv[i], bqkv[i])
                q, k, v = jnp.split(qkv, [KEY_DIM, 2 * KEY_DIM], axis=1)
                q = jax.lax.conv_general_dilated(q, Wdw[i], (1, 1), [(2, 2), (2, 2)], dimension_numbers=('NCHW', 'OIHW', 'NCHW'), feature_group_count=KEY_DIM) + bdw[i][None, :, None, None]
                q = q.reshape(Bw, KEY_DIM, N)
                k = k.reshape(Bw, KEY_DIM, N)
                v = v.reshape(Bw, D, N)
                attn = jnp.einsum('bcn,bcm->bnm', q, k) * SCALE + bias[i]
                attn = jax.nn.softmax(attn, axis=-1)
                feat = jnp.einsum('bdm,bnm->bdn', v, attn).reshape(Bw, D, H, W)
                feats.append(feat)
            out = jnp.concatenate(feats, axis=1)
            return _conv1x1(jax.nn.relu(out), Wproj, bproj)

        def _local_window_attn(src, Wqkv, bqkv, Wdw, bdw, Wproj, bproj, attn_bias):
            B, C, H, W = src.shape
            pad_b = -H % WR
            pad_r = -W % WR
            x = jnp.pad(src, ((0, 0), (0, 0), (0, pad_b), (0, pad_r)))
            pH, pW = (H + pad_b, W + pad_r)
            nH, nW = (pH // WR, pW // WR)
            xw = x.reshape(B, C, nH, WR, nW, WR).transpose(0, 2, 4, 1, 3, 5)
            xw = xw.reshape(B * nH * nW, C, WR, WR)
            yw = _cascaded_attn(xw, Wqkv, bqkv, Wdw, bdw, Wproj, bproj, attn_bias)
            y = yw.reshape(B, nH, nW, C, WR, WR).transpose(0, 3, 1, 4, 2, 5)
            y = y.reshape(B, C, pH, pW)
            return y[:, :, :H, :W]
        key = jax.random.key(seed)
        ks = jax.random.split(key, 12)
        w = 0.02
        return {'src': jax.random.normal(ks[0], (16, 256, 40, 40), jnp.float32), 'Wqkv': jax.random.normal(ks[1], (4, 96, 64), jnp.float32) * w, 'bqkv': jax.random.normal(ks[2], (4, 96), jnp.float32) * w, 'Wdw': jax.random.normal(ks[3], (4, 16, 1, 5, 5), jnp.float32) * w, 'bdw': jax.random.normal(ks[4], (4, 16), jnp.float32) * w, 'Wproj': jax.random.normal(ks[5], (256, 256), jnp.float32) * w, 'bproj': jnp.zeros((256,), jnp.float32), 'attn_bias': jax.random.normal(ks[6], (4, 196), jnp.float32) * w, 'norm1_w': jnp.ones((256,), jnp.float32), 'norm1_b': jnp.zeros((256,), jnp.float32), 'norm2_w': jnp.ones((256,), jnp.float32), 'norm2_b': jnp.zeros((256,), jnp.float32), 'Wfc1': jax.random.normal(ks[7], (2048, 256), jnp.float32) * w, 'bfc1': jnp.zeros((2048,), jnp.float32), 'Wfc2': jax.random.normal(ks[8], (256, 2048), jnp.float32) * w, 'bfc2': jnp.zeros((256,), jnp.float32)}
    _L0_conv_all = _L0_conv_setup()
    _L0_conv_in = {k: v for k, v in _L0_conv_all.items() if k in ('Wqkv', 'bqkv', 'Wdw', 'bdw', 'Wproj', 'bproj', 'attn_bias', 'norm1_w', 'norm1_b', 'norm2_w', 'norm2_b', 'Wfc1', 'bfc1', 'Wfc2', 'bfc2', )}
    del _L0_conv_all

    return {
        "x": x,
        "L0_conv_Wqkv": _L0_conv_in["Wqkv"],
        "L0_conv_bqkv": _L0_conv_in["bqkv"],
        "L0_conv_Wdw": _L0_conv_in["Wdw"],
        "L0_conv_bdw": _L0_conv_in["bdw"],
        "L0_conv_Wproj": _L0_conv_in["Wproj"],
        "L0_conv_bproj": _L0_conv_in["bproj"],
        "L0_conv_attn_bias": _L0_conv_in["attn_bias"],
        "L0_conv_norm1_w": _L0_conv_in["norm1_w"],
        "L0_conv_norm1_b": _L0_conv_in["norm1_b"],
        "L0_conv_norm2_w": _L0_conv_in["norm2_w"],
        "L0_conv_norm2_b": _L0_conv_in["norm2_b"],
        "L0_conv_Wfc1": _L0_conv_in["Wfc1"],
        "L0_conv_bfc1": _L0_conv_in["bfc1"],
        "L0_conv_Wfc2": _L0_conv_in["Wfc2"],
        "L0_conv_bfc2": _L0_conv_in["bfc2"],
    }

def reference(x, L0_conv_Wqkv, L0_conv_bqkv, L0_conv_Wdw, L0_conv_bdw, L0_conv_Wproj, L0_conv_bproj, L0_conv_attn_bias, L0_conv_norm1_w, L0_conv_norm1_b, L0_conv_norm2_w, L0_conv_norm2_b, L0_conv_Wfc1, L0_conv_bfc1, L0_conv_Wfc2, L0_conv_bfc2):
    import jax
    import jax.numpy as jnp
    def _L0_conv_ref(src, Wqkv, bqkv, Wdw, bdw, Wproj, bproj, attn_bias, norm1_w, norm1_b, norm2_w, norm2_b, Wfc1, bfc1, Wfc2, bfc2):
        import jax, jax.numpy as jnp
        import numpy as np
        WR = 14
        KEY_DIM = 16
        D = 64
        NH = 4
        SCALE = KEY_DIM ** (-0.5)
        EPS = 1e-06

        def _bias_idxs(wr):
            pts = [(i, j) for i in range(wr) for j in range(wr)]
            offmap, idxs = ({}, [])
            for p1 in pts:
                for p2 in pts:
                    off = (abs(p1[0] - p2[0]), abs(p1[1] - p2[1]))
                    if off not in offmap:
                        offmap[off] = len(offmap)
                    idxs.append(offmap[off])
            return np.array(idxs, np.int32).reshape(wr * wr, wr * wr)
        BIAS_IDXS = _bias_idxs(WR)

        def _layernorm_cf(x, w, b):
            u = x.mean(1, keepdims=True)
            s = ((x - u) ** 2).mean(1, keepdims=True)
            xn = (x - u) / jnp.sqrt(s + EPS)
            return w[None, :, None, None] * xn + b[None, :, None, None]

        def _conv1x1(x, w, b):
            return jnp.einsum('bchw,oc->bohw', x, w) + b[None, :, None, None]

        def _cascaded_attn(xw, Wqkv, bqkv, Wdw, bdw, Wproj, bproj, attn_bias):
            Bw, C, H, W = xw.shape
            N = H * W
            bias = attn_bias[:, BIAS_IDXS]
            chunks = jnp.split(xw, NH, axis=1)
            feats = []
            feat = chunks[0]
            for i in range(NH):
                if i > 0:
                    feat = feat + chunks[i]
                qkv = _conv1x1(feat, Wqkv[i], bqkv[i])
                q, k, v = jnp.split(qkv, [KEY_DIM, 2 * KEY_DIM], axis=1)
                q = jax.lax.conv_general_dilated(q, Wdw[i], (1, 1), [(2, 2), (2, 2)], dimension_numbers=('NCHW', 'OIHW', 'NCHW'), feature_group_count=KEY_DIM) + bdw[i][None, :, None, None]
                q = q.reshape(Bw, KEY_DIM, N)
                k = k.reshape(Bw, KEY_DIM, N)
                v = v.reshape(Bw, D, N)
                attn = jnp.einsum('bcn,bcm->bnm', q, k) * SCALE + bias[i]
                attn = jax.nn.softmax(attn, axis=-1)
                feat = jnp.einsum('bdm,bnm->bdn', v, attn).reshape(Bw, D, H, W)
                feats.append(feat)
            out = jnp.concatenate(feats, axis=1)
            return _conv1x1(jax.nn.relu(out), Wproj, bproj)

        def _local_window_attn(src, Wqkv, bqkv, Wdw, bdw, Wproj, bproj, attn_bias):
            B, C, H, W = src.shape
            pad_b = -H % WR
            pad_r = -W % WR
            x = jnp.pad(src, ((0, 0), (0, 0), (0, pad_b), (0, pad_r)))
            pH, pW = (H + pad_b, W + pad_r)
            nH, nW = (pH // WR, pW // WR)
            xw = x.reshape(B, C, nH, WR, nW, WR).transpose(0, 2, 4, 1, 3, 5)
            xw = xw.reshape(B * nH * nW, C, WR, WR)
            yw = _cascaded_attn(xw, Wqkv, bqkv, Wdw, bdw, Wproj, bproj, attn_bias)
            y = yw.reshape(B, nH, nW, C, WR, WR).transpose(0, 3, 1, 4, 2, 5)
            y = y.reshape(B, C, pH, pW)
            return y[:, :, :H, :W]
        src2 = _local_window_attn(src, Wqkv, bqkv, Wdw, bdw, Wproj, bproj, attn_bias)
        x = _layernorm_cf(src + src2, norm1_w, norm1_b)
        h = _conv1x1(x, Wfc1, bfc1)
        h = jax.nn.gelu(h, approximate=False)
        h = _conv1x1(h, Wfc2, bfc2)
        return _layernorm_cf(x + h, norm2_w, norm2_b)

    def _gn(v, G=32, eps=1e-5):
        B_, C_, H_, W_ = v.shape
        g = v.reshape(B_, G, C_ // G, H_, W_)
        m = jnp.mean(g, axis=(2, 3, 4), keepdims=True)
        s = jnp.var(g, axis=(2, 3, 4), keepdims=True)
        return ((g - m) / jnp.sqrt(s + eps)).reshape(v.shape)

    def _ln_c(v, eps=1e-6):
        m = jnp.mean(v, axis=1, keepdims=True)
        s = jnp.var(v, axis=1, keepdims=True)
        return (v - m) / jnp.sqrt(s + eps)

    def _ln_t(v, eps=1e-5):
        m = jnp.mean(v, axis=-1, keepdims=True)
        s = jnp.var(v, axis=-1, keepdims=True)
        return (v - m) / jnp.sqrt(s + eps)

    def _to_tokens(v):
        B_, C_, H_, W_ = v.shape
        return v.reshape(B_, C_, H_ * W_).transpose(0, 2, 1)
    def _from_tokens(t, like):
        B_, C_, H_, W_ = like.shape
        return t.transpose(0, 2, 1).reshape(B_, C_, H_, W_)

    x = _L0_conv_ref(x, L0_conv_Wqkv, L0_conv_bqkv, L0_conv_Wdw, L0_conv_bdw, L0_conv_Wproj, L0_conv_bproj, L0_conv_attn_bias, L0_conv_norm1_w, L0_conv_norm1_b, L0_conv_norm2_w, L0_conv_norm2_b, L0_conv_Wfc1, L0_conv_bfc1, L0_conv_Wfc2, L0_conv_bfc2)
    return x


_drawn_inputs = setup_inputs


def setup_inputs(seed=0):
    import zlib

    import numpy as np

    out = dict(_drawn_inputs(seed))
    spreads = {'L0_conv_bproj': (0.0, 0.1),
     'L0_conv_norm1_w': (1.0, 0.2),
     'L0_conv_norm1_b': (0.0, 0.1),
     'L0_conv_norm2_w': (1.0, 0.2),
     'L0_conv_norm2_b': (0.0, 0.1),
     'L0_conv_bfc1': (0.0, 0.1),
     'L0_conv_bfc2': (0.0, 0.1)}
    factors = {'L0_conv_Wqkv': 8.0,
     'L0_conv_bqkv': 8.0,
     'L0_conv_Wdw': 8.0,
     'L0_conv_bdw': 8.0,
     'L0_conv_Wproj': 8.0,
     'L0_conv_attn_bias': 8.0}
    for name, (base, spread) in spreads.items():
        noise = np.random.default_rng([zlib.crc32(name.encode()), seed]).standard_normal(out[name].shape)
        drawn = base * np.exp(spread * noise) if base else spread * noise
        out[name] = jnp.asarray(drawn.astype(out[name].dtype))
    for name, factor in factors.items():
        out[name] = (out[name] * factor).astype(out[name].dtype)
    return out
```

```python
from contextlib import ExitStack

import numpy as np
import concourse.bass as bass
from concourse import mybir

F32 = mybir.dt.float32
F32R = mybir.dt.float32r
ALU = mybir.AluOpType
ACT = mybir.ActivationFunctionType

IMAGES, C, H, W = 16, 256, 40, 40
WR = 14
N = WR * WR
HALF = N // 2
NW = -(-H // WR)
HEADS, KD, D = 4, 16, 64
FF = 2048
SCALE = KD ** -0.5
EPS = 1e-6
PAIRS = 4
P = 128
KT = C // P
FB = FF // P
PADW = WR + 4
TAPS = 25
HRING = 10
BIG = 3.0e38


def positions():
    pos = [(a, b) for a in range(NW) for b in range(NW)]
    kind = lambda ab: (min(WR, H - WR * ab[0]), min(WR, W - WR * ab[1]))
    return sorted(pos, key=lambda ab: (-kind(ab)[0] * kind(ab)[1], -kind(ab)[0])), kind


def kinds():
    pos, kind = positions()
    out = []
    for ab in pos:
        k = kind(ab)
        if out and out[-1][:2] == k:
            out[-1] = (*k, out[-1][2] + 2)
        else:
            out.append((*k, 2))
    return out


KINDS = kinds()
GROUPS = sum(k[2] for k in KINDS)
FIRST = [sum(k[2] for k in KINDS[:j]) for j in range(len(KINDS))]
KIND_OF = [j for j, k in enumerate(KINDS) for _ in range(k[2])]

VEC = {}
for _name, _n in (("bq", HEADS), ("bk", HEADS), ("bv", HEADS), ("bdw", HEADS), ("dw", HEADS * TAPS), ("bproj", KT),
                  ("n1w", KT), ("n1b", KT), ("n2w", KT), ("n2b", KT), ("b1", FB), ("b2", KT), ("lo_rows", 1)):
    VEC[_name] = (sum(n for _, n in VEC.values()), _n)
NVEC = sum(n for _, n in VEC.values())

EARLY = FB - HRING
STEPS = 13
UNITS = 2 * PAIRS
FC2_AT = {0: 1, 1: 1, 2: 1, 3: 1, 4: 1, 5: 1, 6: 1, 8: 1, 10: 1, 12: 1}


class Slot:

    def __init__(self, g, i, static):
        self.g, self.i = g, i
        self.t = g * HEADS + i
        t = static * HEADS + i
        last = GROUPS * HEADS
        self.first = t == 0
        self.attn = t < last
        self.proj = i == 0 and HEADS <= t <= last
        self.ln1 = HEADS <= t < last + 4
        self.mlp = 5 <= t < last + 5
        self.ln2 = 6 <= t < last + 6
        self.st = t
        self.kind1 = KIND_OF[(t - 4) // 4] if self.ln1 else None
        self.kindm = KIND_OF[(t - 5) // 4] if self.mlp else None
        self.kind2 = KIND_OF[(t - 6) // 4] if self.ln2 else None
        self.c1, self.cm, self.c2 = self.t - 4, self.t - 5, self.t - 6


def tokens(kind):
    return 2 * KINDS[kind][0] * KINDS[kind][1]


def program():
    total = GROUPS + 2
    key = lambda g: tuple(KIND_OF[x] if 0 <= x < GROUPS else None for x in (g - 2, g - 1, g)) if g < GROUPS else None
    out, g = [], 0
    while g < total:
        e = g + 1
        while g >= 2 and key(g) is not None and e < total and key(e) == key(g):
            e += 1
        out.append((g, e, e - g >= 2))
        g = e
    return out


def build(nc, xa, xrs, wqkv, bias, w1t, w2t, wpt, vec, ident_in, outs):
    ctx = ExitStack()
    with ctx:
        def sb(name, shape, dt=F32):
            return ctx.enter_context(nc.sbuf_tensor(name, shape, dt))

        def sem(name):
            return ctx.enter_context(nc.semaphore(name))

        TM = 2 * N
        w1h, w1l = (sb(n, [P, KT, FF], F32R) for n in ("w1h", "w1l"))
        w2h, w2l = (sb(n, [P, FB, C], F32R) for n in ("w2h", "w2l"))
        wq = sb("wq", [P, HEADS, PAIRS, P])
        wk = sb("wk", [P, HEADS, P])
        wv = sb("wv", [P, HEADS, P])
        wp = sb("wp", [P, KT, C])
        nbias = sb("nbias", [HALF, HEADS, 2, N])
        vecs = sb("vecs", [P, NVEC])
        dws = sb("dws", [P, HEADS * (TAPS + 1)])
        ident = sb("ident", [P, P])
        mean_w = sb("mean_w", [P, P])
        ones = sb("ones", [P, P])
        minus_half = sb("minus_half", [HALF, 4])
        x_in = [sb(f"x_in{b}", [P, PAIRS, N]) for b in range(2)]
        qpad = sb("qpad", [P, PADW, PADW])
        conv = [sb(f"conv{b}", [P, N]) for b in range(2)]
        q_hi, q_lo = (sb(n, [P, N], F32R) for n in ("q_hi", "q_lo"))
        q_stack = sb("q_stack", [P, PAIRS, N], F32R)
        k_f = sb("k_f", [P, 2, 2 * N])
        k_hi = sb("k_hi", [P, 2 * N], F32R)
        k_stack = sb("k_stack", [P, 2, 2 * N], F32R)
        vt = sb("vt", [HALF, PAIRS, 2, P])
        nscore = [sb(f"nscore{b}", [HALF, 2, N]) for b in range(2)]
        nmax = [sb(f"nmax{b}", [HALF, 2]) for b in range(2)]
        prob = [sb(f"prob{b}", [HALF, 2, N]) for b in range(2)]
        psums = [sb(f"psums{b}", [HALF, 2]) for b in range(2)]
        rsums = [sb(f"rsums{b}", [HALF, 2]) for b in range(2)]
        probt = [sb(f"probt{b}", [HALF, 2, N]) for b in range(2)]
        relu = sb("relu", [P, PAIRS, N])
        proj_in = sb("proj_in", [P, KT, PAIRS, 2, N])
        y = [sb(f"y{p}", [P, KT * TM]) for p in range(PAIRS)]
        z = [sb(f"z{b}", [P, KT * TM]) for b in range(2)]
        z_hi, z_lo = (sb(n, [P, KT * TM], F32R) for n in ("z_hi", "z_lo"))
        h_f = [sb(f"h_f{b}", [P, TM]) for b in range(2)]
        h_hi = sb("h_hi", [P, HRING, TM], F32R)
        h_lo = sb("h_lo", [P, HRING, TM], F32R)
        r = sb("r", [P, KT * TM])
        tsum = sb("tsum", [P, TM])
        sq = sb("sq", [P, KT * TM])
        vcol = sb("vcol", [HALF, 4])
        rcol = sb("rcol", [HALF, 4])
        rdiag = sb("rdiag", [HALF, TM])
        hid = [ctx.enter_context(nc.psum_tensor(f"hid{b}", [P, 512], F32)) for b in range(2)]
        acc = [ctx.enter_context(nc.psum_tensor(f"acc{b}", [P, 512], F32)) for b in range(2)]
        mix = [ctx.enter_context(nc.psum_tensor(f"mix{b}", [P, 512], F32)) for b in range(2)]
        sc = ctx.enter_context(nc.psum_tensor("sc", [P, 512], F32))
        tr = ctx.enter_context(nc.psum_tensor("tr", [P, 512], F32))

        s_const = sem("const_loaded")
        s_gate, v_gate = sem("sync_waited"), sem("vector_waited")
        s_stage = [sem(f"weights_staged{b}") for b in range(PAIRS)]
        s_split_hi = sem("weights_hi_done")
        s_split = sem("weights_split")
        s_set = sem("memsets_done")
        s_setv = sem("vector_consts_done")
        s_xa = [sem(f"x_loaded{b}") for b in range(2)]
        s_xr = [sem(f"residual_loaded{p}") for p in range(PAIRS)]
        s_qst = sem("q_stacked")
        s_rf = sem("relu_moved")
        s_out = sem("out_stored")
        p_q, p_k, p_v = sem("q_product"), sem("k_product"), sem("v_product")
        p_s, p_t, p_o = sem("scores"), sem("transposed"), sem("attended")
        p_proj = sem("projected")
        p_h, p_c = sem("hidden"), sem("fc2_block")
        p_l1, p_l2 = sem("norm1_stats"), sem("norm2_stats")
        a_q, a_k, a_v = sem("q_copied"), sem("k_copied"), sem("v_copied")
        a_g = sem("gelu_done")
        a_e, a_pt, a_r = sem("exp_done"), sem("probt_copied"), sem("relu_done")
        a_sq1, a_sq2 = sem("norm1_squares"), sem("norm2_squares")
        v_s, v_rs, v_p = sem("scores_read"), sem("sums_inverted"), sem("prob_scaled")
        v_f = sem("feat_ready")
        v_conv = sem("conv_steps")
        v_qs = sem("q_split")
        v_kh, v_ks = sem("k_hi_done"), sem("k_stacked")
        v_y = sem("y_ready")
        v_l1, v_l2 = sem("norm1_steps"), sem("norm2_steps")
        g_hl = sem("h_lo_done")
        g_p1, g_p2 = sem("norm1_rsqrt"), sem("norm2_rsqrt")

        def col(name, j=0, rows=slice(0, P)):
            a = VEC[name][0] + j
            return vecs[rows, a:a + 1]

        def kt3(tile, T):
            return tile[:, 0:KT * T].rearrange("p (k n) -> p k n", k=KT)

        def win(ap):
            return ap.rearrange("p (a b) -> p a b", a=WR)

        def run_slots(eng, slot):
            for g0, g1, looped in program():
                if looped:
                    with eng.Fori(g0, g1) as g:
                        for i in range(HEADS):
                            slot(Slot(g, i, g0))
                else:
                    for i in range(HEADS):
                        s = Slot(g0, i, g0)
                        if s.attn or s.ln1 or s.mlp or s.ln2:
                            slot(s)

        block = ctx.enter_context(nc.Block())

        PIECE = 512
        pieces = []
        for src, hi, lo, width in ((w1t, w1h, w1l, KT * FF), (w2t, w2h, w2l, FB * C)):
            fl = [t[:, :, :].rearrange("p a b -> p (a b)") for t in (hi, lo)]
            for c in range(0, width, PIECE):
                pieces.append((src[:, c:c + PIECE], fl[0][:, c:c + PIECE], fl[1][:, c:c + PIECE]))

        @block.sync
        def _(sp):
            def await_(semaphore, value):
                sp.wait_ge(semaphore, value)
                sp.sem_inc(s_gate, 1)

            def load_x(g, i, t_static, g_next):
                b = i % 2
                if t_static >= 2:
                    await_(p_v, g * 8 + 2 * i - 2)
                sp.dma_start(x_in[b][:, :, :], xa[g, :, i]).then_inc(s_xa[b], 16)

            sp.dma_start(vecs[:, :], vec[:, :]).then_inc(s_const, 16)
            sp.dma_start(wq[:, :, :, :].rearrange("p a b c -> p (a b c)"), wqkv[:, 0:HEADS * PAIRS * P]).then_inc(s_const, 16)
            a = HEADS * PAIRS * P
            sp.dma_start(wk[:, :, :].rearrange("p a b -> p (a b)"), wqkv[:, a:a + HEADS * P]).then_inc(s_const, 16)
            sp.dma_start(wv[:, :, :].rearrange("p a b -> p (a b)"), wqkv[:, a + HEADS * P:a + 2 * HEADS * P]).then_inc(s_const, 16)
            load_x(0, 0, 0, 0)
            load_x(0, 1, 1, 0)
            sp.dma_start(nbias[:, :, :, :].rearrange("p a b c -> p (a b c)"), bias[:, :]).then_inc(s_const, 16)
            sp.dma_start(ident[:, :], ident_in[:, :]).then_inc(s_const, 16)
            sp.dma_start(wp[:, :, :].rearrange("p a b -> p (a b)"), wpt[:, :]).then_inc(s_const, 16)
            for n, (src, _, _) in enumerate(pieces):
                if n >= PAIRS:
                    await_(s_split, n - PAIRS + 1)
                sp.dma_start(y[n % PAIRS][:, 0:PIECE], src).then_inc(s_stage[n % PAIRS], 16)
            await_(s_split, len(pieces))
            for p in range(PAIRS):
                sp.dma_start(y[p][:, 0:KT * tokens(0)], xrs[0][0, p]).then_inc(s_xr[p], 16)

            def slot(s):
                g, i, t = s.g, s.i, s.t
                if s.attn:
                    await_(v_qs, t * 2 + 2)
                    if not s.first:
                        await_(p_s, t * 8)
                    for h in range(2):
                        for row, part in enumerate((q_hi, q_lo, q_hi, q_lo)):
                            a = 64 * h + KD * row
                            sp.dma_start(q_stack[a:a + KD, :, :].bitcast(F32),
                                         part[64 * h:64 * h + 64, :].bitcast(F32)).then_inc(s_qst, 16)
                if s.st + 2 < GROUPS * HEADS:
                    t2 = s.st + 2
                    load_x(g + (i + 2) // HEADS, (i + 2) % HEADS, t2, None)
                if s.ln2:
                    await_(v_l2, s.c2 * 10 + 10)
                    g2 = (g - 2) if i < 2 else (g - 1)
                    T = tokens(s.kind2)
                    sp.dma_start(outs[s.kind2][g2 - FIRST[s.kind2], (i - 6) % 4], r[:, 0:KT * T]).then_inc(s_out, 16)
                if s.attn:
                    await_(a_r, t * 4 + 4)
                    if i == 0 and s.st >= HEADS:
                        await_(p_proj, g * 8)
                    for h in range(2):
                        sp.dma_start(proj_in[64 * (i % 2):64 * (i % 2) + 64, i // 2, :, h, :],
                                     relu[64 * h:64 * h + 64, :, :]).then_inc(s_rf, 16)
                if s.ln1 and s.attn:
                    await_(v_l1, s.c1 * 10 + 8)
                    k = KIND_OF[s.st // HEADS]
                    sp.dma_start(y[i][:, 0:KT * tokens(k)], xrs[k][g - FIRST[k], i]).then_inc(s_xr[i], 16)

            run_slots(sp, slot)
            sp.wait_ge(s_out, 16 * GROUPS * PAIRS)

        @block.tensor
        def _(pe):
            pe.wait_ge(s_const, 16 * 7)
            pe.wait_ge(s_set, 4)

            def fc1(s, f):
                T = tokens(s.kindm)
                zh, zl = kt3(z_hi, T), kt3(z_lo, T)
                if f == 0:
                    pe.wait_ge(v_l1, s.cm * 10 + 10)
                if f >= 2:
                    pe.wait_ge(a_g, s.cm * 32 + 2 * (f - 2) + 2)
                elif not s.st == 5:
                    pe.wait_ge(a_g, s.cm * 32)
                n = 0
                for k in range(KT):
                    for w, x in ((w1h, zh), (w1h, zl), (w1l, zh)):
                        mm = pe.matmul(hid[f % 2][:, 0:T], w[:, k, f * P:(f + 1) * P], x[:, k, :],
                                       start=n == 0, stop=n == 3 * KT - 1)
                        n += 1
                mm.then_inc(p_h, 1)

            def fc2(s, f):
                T = tokens(s.kindm)
                if f == 0 and s.st > 5:
                    pe.wait_ge(v_l2, (s.cm - 1) * 10 + 2)
                pe.wait_ge(g_hl, s.cm * 16 + f + 1)
                for c in range(KT):
                    for n, (w, x) in enumerate(((w2h, h_hi), (w2h, h_lo), (w2l, h_hi))):
                        mm = pe.matmul(acc[c][:, 0:T], w[:, f, c * P:(c + 1) * P], x[:, f % HRING, 0:T],
                                       start=f == 0 and n == 0, stop=f == FB - 1 and n == 2)
                mm.then_inc(p_c, 1)

            def stats(s, step, which):
                kind, c, steps, done, banks = ((s.kind1, s.c1, v_l1, p_l1, (hid[0], hid[1], hid[0])) if which == 1
                                               else (s.kind2, s.c2, v_l2, p_l2, (tr, tr, tr)))
                T = tokens(kind)
                q = T // 4
                at = (1, 3, 5) if which == 1 else (3, 5, 7)
                pe.wait_ge(steps, c * 10 + at[step])
                bank = banks[step]
                if step == 0:
                    if which == 1:
                        if s.mlp:
                            pe.wait_ge(a_g, s.cm * 32 + 32)
                    elif s.st <= GROUPS * HEADS:
                        pe.wait_ge(a_pt, s.t * 8)
                    mm = pe.matmul(bank[:, 0:T], mean_w[:, :], tsum[:, 0:T], start=True, stop=True)
                elif step == 1:
                    for j in range(4):
                        mm = pe.matmul(bank[0:q, j:j + 1], tsum[:, q * j:q * j + q], mean_w[:, 0:1], start=True, stop=True)
                else:
                    mm = pe.matmul(bank[:, 0:T], ones[0:q, :], rdiag[0:q, 0:T], start=True, stop=True)
                mm.then_inc(done, 1)

            def proj(s, p):
                k = s.kind1
                rows, cols, _ = KINDS[k]
                T = tokens(k)
                g1 = s.g - 1
                if p == 0:
                    pe.wait_ge(s_rf, s.g * 128)
                    if s.attn:
                        pe.wait_ge(a_v, s.t * 2 + 2)
                    else:
                        pe.wait_ge(a_r, s.t * 4)
                for c in range(KT):
                    if p > 0:
                        pe.wait_ge(v_y, g1 * 8 + 2 * (p - 1) + c + 1)
                    for kk in range(KT):
                        x = proj_in[:, kk, p, :, :].rearrange("p h (a b) -> p h a b", a=WR)[:, :, 0:rows, 0:cols]
                        mm = pe.matmul(mix[c][:, 0:T], wp[:, kk, c * P:(c + 1) * P], x, start=kk == 0, stop=kk == KT - 1)
                    mm.then_inc(p_proj, 1)

            def slot(s):
                g, i, t = s.g, s.i, s.t
                x = x_in[i % 2]

                def q_product():
                    if i == 0:
                        pe.wait_ge(s_xa[0], g * 32 + 16)
                    else:
                        pe.wait_ge(v_f, g * 12 + 4 * i)
                    if not s.first:
                        pe.wait_ge(a_r, t * 4)
                    for p in range(PAIRS):
                        mm = pe.matmul(mix[0][:, 0:N], wq[:, i, p, :], x[:, p, :], start=p == 0, stop=p == PAIRS - 1)
                    mm.then_inc(p_q, 1)

                def k_product(j):
                    if j == 1:
                        pe.wait_ge(a_q, t + 1)
                    pe.matmul(mix[1 - j][:, 0:2 * N], wk[:, i, :], x[:, 2 * j:2 * j + 2, :].rearrange("p a b -> p (a b)"),
                              start=True, stop=True).then_inc(p_k, 1)

                def v_product(j):
                    pe.wait_ge(a_k, t * 2 + j + 1)
                    for p in range(2):
                        for m in range(2):
                            a = (2 * p + m) * P
                            mm = pe.matmul(mix[1 - j][0:HALF, a:a + P], x[:, 2 * j + p, HALF * m:HALF * (m + 1)], wv[:, i, :],
                                           start=True, stop=True)
                    mm.then_inc(p_v, 1)

                def scores(u):
                    p, h = u // 2, u % 2
                    if u == 0:
                        pe.wait_ge(s_qst, t * 128 + 128)
                        pe.wait_ge(v_ks, t * 2 + 2)
                    if u > 0:
                        pe.wait_ge(v_s, t * 8 + u)
                    elif not s.first:
                        pe.wait_ge(v_s, t * 8)
                    a = 64 * h
                    k = k_stack[a:a + 64, p // 2, N * (p % 2):N * (p % 2) + N]
                    for m in range(2):
                        mm = pe.matmul(sc[0:HALF, N * m:N * m + N], q_stack[a:a + 64, p, HALF * m:HALF * m + HALF], k,
                                       start=True, stop=True)
                    mm.then_inc(p_s, 1)

                def transposes(u):
                    pe.wait_ge(v_p, t * 8 + u + 1)
                    if u > 0:
                        pe.wait_ge(a_pt, t * 8 + u)
                    else:
                        if s.ln2:
                            pe.wait_ge(v_l2, s.c2 * 10 + 8)
                        elif not s.first:
                            pe.wait_ge(a_pt, t * 8)
                    for m in range(2):
                        for n in range(2):
                            mm = pe.transpose(tr[0:HALF, N * m + HALF * n:N * m + HALF * (n + 1)],
                                              prob[u % 2][:, n, HALF * m:HALF * (m + 1)], ident[0:HALF, 0:HALF])
                    mm.then_inc(p_t, 1)

                def attend(u):
                    p, h = u // 2, u % 2
                    if u == 0:
                        if s.proj:
                            pe.wait_ge(v_y, g * 8)
                        pe.wait_ge(a_v, t * 2 + 2)
                    if h == 0 and p >= 2:
                        pe.wait_ge(a_r, t * 4 + p - 1)
                    pe.wait_ge(a_pt, t * 8 + u + 1)
                    for m in range(2):
                        mm = pe.matmul(mix[p % 2][64 * h:64 * h + 64, 0:N], vt[:, p, m, 64 * h:64 * h + 64], probt[u % 2][:, m, :],
                                       start=m == 0, stop=m == 1)
                    mm.then_inc(p_o, 1)

                for f in range(FB):
                    if s.mlp:
                        if f >= HRING:
                            fc2(s, f - HRING)
                        fc1(s, f)
                    if s.attn:
                        if f == 0:
                            q_product()
                        if f in (1, 2):
                            k_product(f - 1)
                        if f in (3, 4):
                            v_product(f - 3)
                    if s.ln2 and f in (2, 7, 12):
                        stats(s, (2, 7, 12).index(f), 2)
                    if s.proj and f in (6, 8, 10, 12):
                        proj(s, (f - 6) // 2)
                done = EARLY
                for k in range(STEPS):
                    if s.attn and k < UNITS:
                        scores(k)
                    if s.mlp:
                        for _ in range(FC2_AT.get(k, 0)):
                            fc2(s, done)
                            done += 1
                    if s.ln1 and k in (1, 5, 9):
                        stats(s, (1, 5, 9).index(k), 1)
                    if s.attn and 0 <= k - 3 < UNITS:
                        transposes(k - 3)
                    if s.attn and 0 <= k - 5 < UNITS:
                        attend(k - 5)

            run_slots(pe, slot)

        @block.scalar
        def _(act):
            act.wait_ge(s_const, 16 * 7)
            act.wait_ge(s_set, 4)

            def gelu(s, f):
                T = tokens(s.kindm)
                act.wait_ge(p_h, s.cm * 16 + f + 1)
                act.activation(h_hi[:, f % HRING, 0:T], hid[f % 2][:, 0:T], ACT.Gelu, bias=col("b1", f)).then_inc(a_g, 1)
                if s.st > 5 or f >= 2:
                    act.wait_ge(g_hl, s.cm * 16 + f - 1)
                act.activation(h_f[f % 2][:, 0:T], hid[f % 2][:, 0:T], ACT.Gelu, bias=col("b1", f)).then_inc(a_g, 1)

            def square(s, which):
                kind, c, steps, src, done, at = ((s.kind1, s.c1, v_l1, y[s.i], a_sq1, 2) if which == 1
                                                 else (s.kind2, s.c2, v_l2, r, a_sq2, 4))
                n = KT * tokens(kind)
                act.wait_ge(steps, c * 10 + at)
                act.activation(sq[:, 0:n], src[:, 0:n], ACT.Square).then_inc(done, 1)

            def slot(s):
                g, i, t = s.g, s.i, s.t
                for f in range(FB):
                    if s.mlp:
                        gelu(s, f)
                    if s.attn:
                        if f == 0:
                            act.wait_ge(p_q, t + 1)
                            if not s.first:
                                act.wait_ge(v_conv, t * 26)
                            act.activation(qpad[:, 2:2 + WR, 2:2 + WR], win(mix[0][:, 0:N]), ACT.Identity,
                                           bias=col("bq", i)).then_inc(a_q, 1)
                        if f in (1, 2):
                            j = f - 1
                            act.wait_ge(p_k, t * 2 + j + 1)
                            if not s.first:
                                act.wait_ge(v_ks, t * 2 + j - 1)
                            act.activation(k_f[:, j, :], mix[1 - j][:, 0:2 * N], ACT.Identity, bias=col("bk", i)).then_inc(a_k, 1)
                        if f in (3, 4):
                            j = f - 3
                            act.wait_ge(p_v, t * 2 + j + 1)
                            act.activation(vt[:, 2 * j:2 * j + 2, :, :].rearrange("p a b c -> p (a b c)"), mix[1 - j][0:HALF, :],
                                           ACT.Copy).then_inc(a_v, 1)
                    if s.ln2 and f == 5:
                        square(s, 2)
                for k in range(STEPS + 1):
                    u = k - 1
                    if s.attn and 0 <= u < UNITS:
                        b = u % 2
                        act.wait_ge(v_s, t * 8 + u + 1)
                        if u >= 2:
                            act.wait_ge(p_t, t * 8 + u - 1)
                        elif not s.first:
                            act.wait_ge(p_t, t * 8)
                        for m in range(2):
                            e = act.activation(prob[b][:, m, :], nscore[b][:, m, :], ACT.Exp, bias=nmax[b][:, m:m + 1],
                                               scale=-1.0, accum_out=psums[b][:, m:m + 1])
                        e.then_inc(a_e, 1)
                    if s.ln1 and k == 3:
                        square(s, 1)
                    u = k - 3
                    if s.attn and 0 <= u < UNITS:
                        act.wait_ge(p_t, t * 8 + u + 1)
                        if u >= 2:
                            act.wait_ge(p_o, t * 8 + u - 1)
                        act.activation(probt[u % 2][:, :, :].rearrange("p a b -> p (a b)"), tr[0:HALF, 0:2 * N],
                                       ACT.Copy).then_inc(a_pt, 1)
                    if s.attn and k >= 6 and k % 2 == 0 and (k - 6) // 2 < PAIRS or s.attn and k == STEPS:
                        for p in ([(k - 6) // 2] if k < 12 else [3] if k == 12 else []):
                            act.wait_ge(p_o, t * 8 + 2 * p + 2)
                            if p == 0 and not s.first:
                                act.wait_ge(s_rf, t * 32)
                            if i < HEADS - 1:
                                act.wait_ge(v_f, g * 12 + 4 * i + p + 1)
                            act.activation(relu[:, p, :], mix[p % 2][:, 0:N], ACT.Relu, bias=col("bv", i)).then_inc(a_r, 1)

            run_slots(act, slot)

        @block.vector
        def _(dve):
            dve.wait_ge(s_const, 16 * 7)
            dve.memset(mean_w[:, :], 1.0 / C).then_inc(s_set, 1)
            dve.memset(ones[:, :], 1.0).then_inc(s_set, 1)
            dve.memset(qpad[:, :, :], 0.0).then_inc(s_set, 1)
            dve.memset(minus_half[:, :], -0.5).then_inc(s_set, 1)
            nb = nbias[:, :, :, :].rearrange("p a b c -> p (a b c)")
            dve.tensor_scalar(nb, nb, -1.0, None, ALU.mult).then_inc(s_setv, 1)
            a = VEC["dw"][0]
            dve.tensor_scalar(dws[:, 0:HEADS * TAPS], vecs[:, a:a + HEADS * TAPS], -SCALE, None, ALU.mult).then_inc(s_setv, 1)
            a = VEC["bdw"][0]
            dve.tensor_scalar(dws[:, HEADS * TAPS:], vecs[:, a:a + HEADS], -SCALE, None, ALU.mult).then_inc(s_setv, 1)
            dve.wait_ge(s_setv, 3)

            def norm(s, step, which):
                kind, c, sem_, stat, sqs, pw, src, base, names = (
                    (s.kind1, s.c1, v_l1, p_l1, a_sq1, g_p1, y[s.i], 0, ("n1w", "n1b")) if which == 1
                    else (s.kind2, s.c2, v_l2, p_l2, a_sq2, g_p2, r, 2, ("n2w", "n2b")))
                T = tokens(kind)
                q = T // 4
                banks = (hid[0], hid[1], hid[0]) if which == 1 else (tr, tr, tr)
                v = kt3(src, T)
                s3 = kt3(sq, T)
                if step > 0 or which == 2:
                    dve.wait_ge(sem_, c * 10 + base + step)
                if step == 0:
                    ins = dve.tensor_tensor(tsum[:, 0:T], v[:, 0, :], v[:, 1, :], ALU.add)
                elif step == 1:
                    dve.wait_ge(stat, c * 3 + 1)
                    ins = dve.tensor_tensor(v, v, banks[0][:, 0:T].unsqueeze(1).broadcast_to([P, KT, T]), ALU.subtract)
                elif step == 2:
                    dve.wait_ge(sqs, c + 1)
                    ins = dve.tensor_tensor(tsum[:, 0:T], s3[:, 0, :], s3[:, 1, :], ALU.add)
                elif step == 3:
                    dve.wait_ge(stat, c * 3 + 2)
                    ins = dve.tensor_scalar(vcol[0:q, :], banks[1][0:q, 0:4], EPS, None, ALU.add)
                elif step == 4:
                    dve.wait_ge(pw, c + 1)
                    ins = dve.tensor_tensor(rdiag[0:q, 0:T].rearrange("p (j n) -> p j n", j=4),
                                            ident[0:q, 0:q].unsqueeze(1).broadcast_to([q, 4, q]),
                                            rcol[0:q, :].unsqueeze(2).broadcast_to([q, 4, q]), ALU.mult)
                elif step == 5:
                    dve.wait_ge(stat, c * 3 + 3)
                    ins = dve.tensor_tensor(v, v, banks[2][:, 0:T].unsqueeze(1).broadcast_to([P, KT, T]), ALU.mult)
                else:
                    k = step - 6
                    dst = kt3(z[(s.i) % 2], T) if which == 1 else v
                    ins = dve.tensor_scalar(dst[:, k, :], v[:, k, :], col(names[0], k), col(names[1], k), ALU.mult, ALU.add)
                ins.then_inc(sem_, 1)

            def slot(s):
                g, i, t = s.g, s.i, s.t

                def read_sums():
                    T = tokens(s.kind2)
                    dve.wait_ge(p_c, s.c2 * 16 + 16)
                    if s.st > 6:
                        dve.wait_ge(s_out, s.c2 * 16)
                    for c in range(KT):
                        dve.scalar_tensor_tensor(kt3(r, T)[:, c, :], acc[c][:, 0:T], col("b2", c), kt3(z[i % 2], T)[:, c, :],
                                                 ALU.add, ALU.add).then_inc(v_l2, 1)

                def conv_steps(a, b):
                    if a == 0:
                        dve.wait_ge(a_q, t + 1)
                    for k in range(a, b):
                        if k >= 2:
                            dve.wait_ge(v_conv, t * 26 + (k - 1 if k < TAPS else TAPS))
                        out = conv[k % 2][:, :]
                        if k == TAPS:
                            ins = dve.tensor_tensor(conv[0][:, :], conv[0][:, :], conv[1][:, :], ALU.add)
                        else:
                            x = qpad[:, k // 5:k // 5 + WR, k % 5:k % 5 + WR]
                            w = dws[:, i * TAPS + k:i * TAPS + k + 1]
                            if k == 0:
                                ins = dve.tensor_scalar(win(out), x, w, dws[:, HEADS * TAPS + i:HEADS * TAPS + i + 1],
                                                        ALU.mult, ALU.add)
                            elif k == 1:
                                ins = dve.tensor_scalar(win(out), x, w, None, ALU.mult)
                            else:
                                ins = dve.scalar_tensor_tensor(win(out), x, w, win(out), ALU.mult, ALU.add)
                        ins.then_inc(v_conv, 1)

                def k_split(j):
                    dve.wait_ge(a_k, t * 2 + j + 1)
                    if not (s.first and j == 0):
                        dve.wait_ge(v_ks, t * 2 + j)
                    dve.tensor_copy(k_hi[:, :], k_f[:, j, :]).then_inc(v_kh, 1)
                    dve.wait_ge(v_kh, t * 2 + j + 1)
                    dve.scalar_tensor_tensor(k_stack[:, j, :], k_hi[:, :].bitcast(F32), col("lo_rows"), k_f[:, j, :],
                                             ALU.mult, ALU.add).then_inc(v_ks, 1)

                def q_split():
                    dve.wait_ge(v_conv, t * 26 + 26)
                    if not s.first:
                        dve.wait_ge(s_qst, t * 128)
                    dve.tensor_copy(q_hi[:, :], conv[0][:, :]).then_inc(v_qs, 1)
                    dve.wait_ge(v_qs, t * 2 + 1)
                    dve.tensor_tensor(q_lo[:, :], conv[0][:, :], q_hi[:, :].bitcast(F32), ALU.subtract).then_inc(v_qs, 1)

                def add_proj(p):
                    g1 = g - 1
                    T = tokens(s.kind1)
                    for c in range(KT):
                        dve.wait_ge(p_proj, g1 * 8 + 2 * p + c + 1)
                        if c == 0:
                            dve.wait_ge(s_xr[p], g * 16)
                        yc = kt3(y[p], T)[:, c, :]
                        dve.scalar_tensor_tensor(yc, mix[c][:, 0:T], col("bproj", c), yc, ALU.add, ALU.add).then_inc(v_y, 1)

                def scores_read(u):
                    b = u % 2
                    dve.wait_ge(p_s, t * 8 + u + 1)
                    if u >= 2:
                        dve.wait_ge(a_e, t * 8 + u - 1)
                    elif not s.first:
                        dve.wait_ge(a_e, t * 8)
                    if u >= 2 or not s.first:
                        dve.wait_ge(v_s, t * 8 + u - 1)
                    dve.sem_inc(v_gate, 1)
                    for m in range(2):
                        ins = dve.tensor_tensor_reduce(nscore[b][:, m, :], sc[0:HALF, N * m:N * m + N], nbias[:, i, m, :],
                                                       1.0, BIG, ALU.add, ALU.min, nmax[b][:, m:m + 1])
                    ins.then_inc(v_s, 1)

                def prob_scale(u):
                    b = u % 2
                    dve.wait_ge(a_e, t * 8 + u + 1)
                    dve.reciprocal(rsums[b][:, :], psums[b][:, :]).then_inc(v_rs, 1)
                    dve.wait_ge(v_rs, t * 8 + u + 1)
                    for m in range(2):
                        ins = dve.tensor_scalar(prob[b][:, m, :], prob[b][:, m, :], rsums[b][:, m:m + 1], None, ALU.mult)
                    ins.then_inc(v_p, 1)

                def next_feat(p):
                    dve.wait_ge(p_o, t * 8 + 2 * p + 2)
                    if p == 0:
                        b = (i + 1) % 2
                        dve.wait_ge(s_xa[b], g * 32 + 16 * ((i + 1) // 2 + 1))
                    dve.scalar_tensor_tensor(x_in[(i + 1) % 2][:, p, :], mix[p % 2][:, 0:N], col("bv", i),
                                             x_in[(i + 1) % 2][:, p, :], ALU.add, ALU.add).then_inc(v_f, 1)

                def split_z(lo):
                    T = tokens(s.kind1)
                    n = KT * T
                    dve.wait_ge(v_l1, s.c1 * 10 + 8 + lo)
                    zz = z[i % 2]
                    if not lo:
                        if s.mlp:
                            dve.wait_ge(p_h, s.cm * 16 + 16)
                        dve.tensor_copy(z_hi[:, 0:n], zz[:, 0:n]).then_inc(v_l1, 1)
                    else:
                        dve.tensor_tensor(z_lo[:, 0:n], zz[:, 0:n], z_hi[:, 0:n].bitcast(F32), ALU.subtract).then_inc(v_l1, 1)

                on = s.attn
                if s.ln2:
                    read_sums()
                    norm(s, 0, 2)
                on and conv_steps(0, 4)
                on and k_split(0)
                s.ln2 and norm(s, 1, 2)
                on and conv_steps(4, 10)
                on and k_split(1)
                s.ln2 and norm(s, 2, 2)
                on and conv_steps(10, 16)
                s.proj and add_proj(0)
                s.ln2 and norm(s, 3, 2)
                on and conv_steps(16, 19)
                s.proj and add_proj(1)
                on and conv_steps(19, 23)
                s.ln2 and norm(s, 4, 2)
                s.proj and add_proj(2)
                on and conv_steps(23, 26)
                on and q_split()
                if s.ln2:
                    norm(s, 5, 2)
                    norm(s, 6, 2)
                    norm(s, 7, 2)
                s.proj and add_proj(3)
                for k in range(STEPS + 1):
                    if on and k < UNITS:
                        scores_read(k)
                    if s.ln1:
                        if k == 0:
                            if i == 0:
                                dve.wait_ge(v_y, g * 8)
                            norm(s, 0, 1)
                        for at, step in ((2, 1), (4, 2), (5, 3), (7, 4), (10, 5), (10, 6), (10, 7)):
                            if k == at:
                                norm(s, step, 1)
                        if k == 11:
                            split_z(0)
                            split_z(1)
                    if on and 0 <= k - 2 < UNITS:
                        prob_scale(k - 2)
                    if on and i < HEADS - 1 and k in (6, 8, 10, 12):
                        next_feat((k - 6) // 2)

            run_slots(dve, slot)

        @block.gpsimd
        def _(pool):
            for n, (_, hi, lo) in enumerate(pieces):
                src = y[n % PAIRS][:, 0:PIECE]
                pool.wait_ge(s_stage[n % PAIRS], 16 * (n // PAIRS + 1))
                pool.tensor_copy(hi, src).then_inc(s_split_hi, 1)
                pool.wait_ge(s_split_hi, n + 1)
                pool.tensor_tensor(lo, src, hi.bitcast(F32), ALU.subtract).then_inc(s_split, 1)
            pool.wait_ge(s_split, len(pieces))
            pool.wait_ge(s_set, 4)

            def rsqrt(s, which):
                kind, c, steps, done, at = ((s.kind1, s.c1, v_l1, g_p1, 4) if which == 1 else (s.kind2, s.c2, v_l2, g_p2, 6))
                q = tokens(kind) // 4
                pool.wait_ge(steps, c * 10 + at)
                pool.tensor_tensor(rcol[0:q, :], vcol[0:q, :], minus_half[0:q, :], ALU.pow).then_inc(done, 1)

            def slot(s):
                for f in range(FB):
                    if s.mlp:
                        T = tokens(s.kindm)
                        pool.wait_ge(a_g, s.cm * 32 + 2 * f + 2)
                        pool.tensor_tensor(h_lo[:, f % HRING, 0:T], h_f[f % 2][:, 0:T], h_hi[:, f % HRING, 0:T].bitcast(F32),
                                           ALU.subtract).then_inc(g_hl, 1)
                    if s.ln2 and f == 8:
                        rsqrt(s, 2)
                if s.ln1:
                    rsqrt(s, 1)

            run_slots(pool, slot)


def _device(nc, in_shapes):
    aps = {n: nc.dram_tensor(f"in_{n}", s, F32, kind="ExternalInput").ap() for n, s in in_shapes.items()}
    outs = []
    for k, (rows, cols, n) in enumerate(KINDS):
        outs.append(nc.dram_tensor(f"out{k}", (n, PAIRS, P, KT * 2 * rows * cols), F32, kind="ExternalOutput").ap())
    build(nc, aps["xa"], [aps[f"xr{k}"] for k in range(len(KINDS))], aps["wqkv"], aps["bias"], aps["w1t"], aps["w2t"],
          aps["wpt"], aps["vec"], aps["ident"], outs)


def kernel(x, L0_conv_Wqkv, L0_conv_bqkv, L0_conv_Wdw, L0_conv_bdw, L0_conv_Wproj, L0_conv_bproj, L0_conv_attn_bias,
           L0_conv_norm1_w, L0_conv_norm1_b, L0_conv_norm2_w, L0_conv_norm2_b, L0_conv_Wfc1, L0_conv_bfc1,
           L0_conv_Wfc2, L0_conv_bfc2):
    import concourse.bacc as _bacc
    from concourse.bass_utils import run_bass_kernel_spmd as _run

    x = np.ascontiguousarray(x)
    f32 = x.dtype
    pos, kind = positions()
    xp = np.zeros((IMAGES, C, NW * WR, NW * WR), f32)
    xp[:, :, :H, :W] = x
    arrays = {}
    xa = np.zeros((GROUPS, P, HEADS, PAIRS, N), f32)
    xrs = [np.zeros((n, PAIRS, P, KT, 2, rows, cols), f32) for rows, cols, n in KINDS]
    for g in range(GROUPS):
        (a, b), half = pos[g // 2], g % 2
        w = xp[8 * half:8 * half + 8, :, WR * a:WR * a + WR, WR * b:WR * b + WR].reshape(2, PAIRS, HEADS, D, N)
        xa[g] = w.transpose(0, 3, 2, 1, 4).reshape(P, HEADS, PAIRS, N)
        k = KIND_OF[g]
        rows, cols, _ = KINDS[k]
        w = xp[8 * half:8 * half + 8, :, WR * a:WR * a + rows, WR * b:WR * b + cols].reshape(2, PAIRS, KT, P, rows, cols)
        xrs[k][g - FIRST[k]] = w.transpose(1, 3, 2, 0, 4, 5)
    arrays["xa"] = xa
    for k, a in enumerate(xrs):
        arrays[f"xr{k}"] = a.reshape(a.shape[0], PAIRS, P, -1)

    wqkv = np.asarray(L0_conv_Wqkv)
    wq = np.zeros((2, D, HEADS, PAIRS, 2, KD, PAIRS), f32)
    wk = np.zeros((2, D, HEADS, 2, 4, KD), f32)
    wv = np.zeros((2, D, HEADS, 2, D), f32)
    for h in range(2):
        for i in range(HEADS):
            for p in range(PAIRS):
                wq[h, :, i, p, h, :, p] = wqkv[i, 0:KD].T
            for c in range(4):
                wk[h, :, i, h, c] = wqkv[i, KD:2 * KD].T
            wv[h, :, i, h] = wqkv[i, 2 * KD:].T
    arrays["wqkv"] = np.concatenate([wq.reshape(P, -1), wk.reshape(P, -1), wv.reshape(P, -1)], 1)

    dist = np.abs(np.arange(WR)[:, None] - np.arange(WR)[None, :])
    idx = (dist[:, None, :, None] * WR + dist[None, :, None, :]).reshape(N, N)
    bias = np.asarray(L0_conv_attn_bias)[:, idx]
    arrays["bias"] = np.ascontiguousarray(bias.reshape(HEADS, 2, HALF, N).transpose(2, 0, 1, 3).reshape(HALF, -1))
    arrays["w1t"] = np.ascontiguousarray(np.asarray(L0_conv_Wfc1).T.reshape(KT, P, FF).transpose(1, 0, 2).reshape(P, -1))
    arrays["w2t"] = np.ascontiguousarray(np.asarray(L0_conv_Wfc2).T.reshape(FB, P, C).transpose(1, 0, 2).reshape(P, -1))
    arrays["wpt"] = np.ascontiguousarray(np.asarray(L0_conv_Wproj).T.reshape(KT, P, C).transpose(1, 0, 2).reshape(P, -1))

    bqkv = np.asarray(L0_conv_bqkv)
    rep = lambda a, n: np.tile(a.T, (n, 1))
    rep_q = lambda a: np.tile(np.repeat(a.T, PAIRS, 0), (2, 1))
    tile = lambda a, n: np.ascontiguousarray(np.asarray(a).reshape(n, P).T)
    lo_rows = np.zeros((2, 4, KD, 1), f32)
    lo_rows[:, 2:] = -1.0
    parts = {
        "bq": rep_q(bqkv[:, 0:KD]), "bk": rep(bqkv[:, KD:2 * KD], 8), "bv": rep(bqkv[:, 2 * KD:], 2),
        "bdw": rep_q(np.asarray(L0_conv_bdw)),
        "dw": rep_q(np.asarray(L0_conv_Wdw).reshape(HEADS, KD, TAPS).transpose(0, 2, 1).reshape(-1, KD)),
        "bproj": tile(L0_conv_bproj, KT), "n1w": tile(L0_conv_norm1_w, KT), "n1b": tile(L0_conv_norm1_b, KT),
        "n2w": tile(L0_conv_norm2_w, KT), "n2b": tile(L0_conv_norm2_b, KT), "b1": tile(L0_conv_bfc1, FB),
        "b2": tile(L0_conv_bfc2, KT), "lo_rows": lo_rows.reshape(P, 1),
    }
    arrays["vec"] = np.ascontiguousarray(np.concatenate([parts[n] for n in VEC], 1))
    arrays["ident"] = np.eye(P, dtype=f32)

    nc = _bacc.Bacc("TRN2", target_bir_lowering=False, num_devices=1)
    _device(nc, {n: a.shape for n, a in arrays.items()})
    res = _run(nc, [{f"in_{n}": a for n, a in arrays.items()}], core_ids=[0]).results[0]

    out = np.zeros((IMAGES, C, H, W), f32)
    for g in range(GROUPS):
        (a, b), half = pos[g // 2], g % 2
        k = KIND_OF[g]
        rows, cols, _ = KINDS[k]
        w = res[f"out{k}"][g - FIRST[k]].reshape(PAIRS, P, KT, 2, rows, cols).transpose(3, 0, 2, 1, 4, 5)
        out[8 * half:8 * half + 8, :, WR * a:WR * a + rows, WR * b:WR * b + cols] = w.reshape(8, C, rows, cols)
    return out
```

```python
from contextlib import ExitStack

import numpy as np
import concourse.bass as bass
from concourse import mybir

F32 = mybir.dt.float32
F32R = mybir.dt.float32r
ALU = mybir.AluOpType
ACT = mybir.ActivationFunctionType

IMAGES, C, H, W = 16, 256, 40, 40
WR = 14
N = WR * WR
HALF = N // 2
NW = -(-H // WR)
HEADS, KD, D = 4, 16, 64
FF = 2048
SCALE = KD ** -0.5
EPS = 1e-6
PAIRS = 4
P = 128
KT = C // P
FB = FF // P
PADW = WR + 4
TAPS = 25
HRING = 12
BIG = 3.0e38


def positions():
    pos = [(a, b) for a in range(NW) for b in range(NW)]
    kind = lambda ab: (min(WR, H - WR * ab[0]), min(WR, W - WR * ab[1]))
    return sorted(pos, key=lambda ab: (-kind(ab)[0] * kind(ab)[1], -kind(ab)[0])), kind


def kinds():
    pos, kind = positions()
    out = []
    for ab in pos:
        k = kind(ab)
        if out and out[-1][:2] == k:
            out[-1] = (*k, out[-1][2] + 2)
        else:
            out.append((*k, 2))
    return out


KINDS = kinds()
GROUPS = sum(k[2] for k in KINDS)
FIRST = [sum(k[2] for k in KINDS[:j]) for j in range(len(KINDS))]
KIND_OF = [j for j, k in enumerate(KINDS) for _ in range(k[2])]

VEC = {}
for _name, _n in (("bq", HEADS), ("bk", HEADS), ("bv", HEADS), ("bdw", HEADS), ("dw", HEADS * TAPS), ("bproj", KT),
                  ("n1w", KT), ("n1b", KT), ("n2w", KT), ("n2b", KT), ("b1", FB), ("b2", KT), ("lo_rows", 1)):
    VEC[_name] = (sum(n for _, n in VEC.values()), _n)
NVEC = sum(n for _, n in VEC.values())

EARLY = FB - HRING
STEPS = 13
UNITS = 2 * PAIRS
FC2_AT = {k: 1 for k in range(12)}
TURNS = 2 * HEADS
SETS = GROUPS // 2
LAST = SETS * TURNS
Q_AT, K_AT, V_AT, PROJ_AT = 1, (2, 3), (4, 5), 7
N2_AT, N1_AT = (2, 5, 8), (10, 13, 15)
SQ2_AT, SQ1_AT = 3, 11


class Slot:

    def __init__(self, g, j, static):
        self.set, self.j = g, j
        self.t = g * TURNS + j
        t = self.st = static * TURNS + j
        self.front = t < LAST
        self.back = 1 <= t <= LAST
        self.ln1 = TURNS <= t < LAST + TURNS
        self.mlp = TURNS + 1 <= t < LAST + TURNS + 1
        self.ln2 = TURNS + 2 <= t < LAST + TURNS + 2
        self.any = self.front or self.back or self.ln1 or self.mlp or self.ln2
        kind = lambda on, c: KIND_OF[2 * (c // TURNS)] if on else None
        self.kind1, self.kindm, self.kind2 = kind(self.ln1, t - 8), kind(self.mlp, t - 9), kind(self.ln2, t - 10)
        self.c1, self.cm, self.c2 = self.t - 8, self.t - 9, self.t - 10
        self.head = j // 2
        self.bt = self.t - 1
        self.bj = (j - 1) % TURNS
        self.bhead = self.bj // 2
        self.bset = g if j else g - 1


def tokens(kind):
    return 2 * KINDS[kind][0] * KINDS[kind][1]


def program():
    total = SETS + 2
    kind = lambda g: KIND_OF[2 * g]
    same = lambda g: 2 <= g < SETS and kind(g - 2) == kind(g - 1) == kind(g)
    out, g = [], 0
    while g < total:
        e = g + 1
        while same(g) and same(e) and kind(e) == kind(g):
            e += 1
        out.append((g, e, e - g >= 2))
        g = e
    return out


def build(nc, xa, relu_d, xrs, wqkv, bias, w1t, w2t, wpt, vec, ident_in, outs):
    ctx = ExitStack()
    with ctx:
        def sb(name, shape, dt=F32):
            return ctx.enter_context(nc.sbuf_tensor(name, shape, dt))

        def sem(name):
            return ctx.enter_context(nc.semaphore(name))

        TM = 2 * N
        w1h, w1l = (sb(n, [P, KT, FF], F32R) for n in ("w1h", "w1l"))
        w2h, w2l = (sb(n, [P, FB, C], F32R) for n in ("w2h", "w2l"))
        wq = sb("wq", [P, HEADS, P + PAIRS - 1])
        wk = sb("wk", [P, HEADS, P])
        wv = sb("wv", [P, HEADS, P])
        wp = sb("wp", [P, KT, C])
        nbias = sb("nbias", [HALF, HEADS, 2, N])
        vecs = sb("vecs", [P, NVEC])
        dws = sb("dws", [P, HEADS * (TAPS + 1)])
        ident = sb("ident", [P, P])
        mean_w = sb("mean_w", [P, P])
        ones = sb("ones", [P, P])
        minus_half = sb("minus_half", [HALF, 4])
        x_in = [sb(f"x_in{b}", [P, PAIRS, N]) for b in range(2)]
        qpad = sb("qpad", [P, PADW, PADW])
        conv = [sb(f"conv{b}", [P, N]) for b in range(2)]
        q_hi, q_lo = (sb(n, [P, N], F32R) for n in ("q_hi", "q_lo"))
        q_stack = [sb(f"q_stack{b}", [P, PAIRS, N], F32R) for b in range(2)]
        k_f = sb("k_f", [P, 2 * N])
        k_hi = sb("k_hi", [P, 2 * N], F32R)
        k_stack = [sb(f"k_stack{b}", [P, 2, 2 * N], F32R) for b in range(2)]
        vt = [sb(f"vt{b}", [HALF, PAIRS, 2, P]) for b in range(2)]
        nscore = [sb(f"nscore{b}", [HALF, 2, N]) for b in range(2)]
        nmax = [sb(f"nmax{b}", [HALF, 2]) for b in range(2)]
        prob = [sb(f"prob{b}", [HALF, 2, N]) for b in range(3)]
        psums = [sb(f"psums{b}", [HALF, 2]) for b in range(3)]
        rsums = [sb(f"rsums{b}", [HALF, 2]) for b in range(3)]
        probt = [sb(f"probt{b}", [HALF, 2, N]) for b in range(2)]
        relu = sb("relu", [P, PAIRS, N])
        proj_in = [sb(f"proj_in{b}", [P, KT, 2, N]) for b in range(2)]
        y = [sb(f"y{b}", [P, KT * TM]) for b in range(2)]
        z = [sb(f"z{b}", [P, KT * TM]) for b in range(2)]
        z_hi, z_lo = (sb(n, [P, KT * TM], F32R) for n in ("z_hi", "z_lo"))
        h_f = [sb(f"h_f{b}", [P, TM]) for b in range(2)]
        h_hi = sb("h_hi", [P, HRING, TM], F32R)
        h_lo = sb("h_lo", [P, HRING, TM], F32R)
        r = sb("r", [P, KT * TM])
        tsum = sb("tsum", [P, TM])
        sq = sb("sq", [P, KT * TM])
        vcol = sb("vcol", [HALF, 4])
        rcol = sb("rcol", [HALF, 4])
        rdiag = sb("rdiag", [HALF, TM])
        hid = [ctx.enter_context(nc.psum_tensor(f"hid{b}", [P, 512], F32)) for b in range(2)]
        acc = [ctx.enter_context(nc.psum_tensor(f"acc{b}", [P, 512], F32)) for b in range(2)]
        mix = [ctx.enter_context(nc.psum_tensor(f"mix{b}", [P, 512], F32)) for b in range(2)]
        sc = ctx.enter_context(nc.psum_tensor("sc", [P, 512], F32))
        tr = ctx.enter_context(nc.psum_tensor("tr", [P, 512], F32))

        s_const = sem("const_loaded")
        s_gate, v_gate = sem("sync_waited"), sem("vector_waited")
        s_stage = [sem(f"weights_staged{b}") for b in range(2)]
        s_split_hi = sem("weights_hi_done")
        s_split = sem("weights_split")
        s_set = sem("memsets_done")
        s_setv = sem("vector_consts_done")
        s_xa = [sem(f"x_loaded{b}") for b in range(2)]
        s_xr = [sem(f"residual_loaded{b}") for b in range(2)]
        s_pin = [sem(f"proj_input_loaded{b}") for b in range(2)]
        s_qst = sem("q_stacked")
        s_rf = sem("relu_stored")
        s_out = sem("out_stored")
        p_q, p_k, p_v = sem("q_product"), sem("k_product"), sem("v_product")
        p_s, p_t, p_o = sem("scores"), sem("transposed"), sem("attended")
        p_proj = sem("projected")
        p_h, p_c = sem("hidden"), sem("fc2_block")
        p_l1, p_l2 = sem("norm1_stats"), sem("norm2_stats")
        a_q, a_k, a_v = sem("q_copied"), sem("k_copied"), sem("v_copied")
        a_g = sem("gelu_done")
        a_e, a_pt, a_r = sem("exp_done"), sem("probt_copied"), sem("relu_done")
        a_sq1, a_sq2 = sem("norm1_squares"), sem("norm2_squares")
        v_s, v_rs, v_p = sem("scores_read"), sem("sums_inverted"), sem("prob_scaled")
        v_f = sem("feat_ready")
        v_conv = sem("conv_steps")
        v_qs = sem("q_split")
        v_kh, v_ks = sem("k_hi_done"), sem("k_stacked")
        v_y = sem("y_ready")
        v_l1, v_l2 = sem("norm1_steps"), sem("norm2_steps")
        g_hl = sem("h_lo_done")
        g_p1, g_p2 = sem("norm1_rsqrt"), sem("norm2_rsqrt")

        def col(name, j=0, rows=slice(0, P)):
            a = VEC[name][0] + j
            return vecs[rows, a:a + 1]

        def kt3(tile, T):
            return tile[:, 0:KT * T].rearrange("p (k n) -> p k n", k=KT)

        def win(ap):
            return ap.rearrange("p (a b) -> p a b", a=WR)

        def run_slots(eng, slot):
            for g0, g1, looped in program():
                if looped:
                    with eng.Fori(g0, g1) as g:
                        for j in range(TURNS):
                            slot(Slot(g, j, g0))
                else:
                    for j in range(TURNS):
                        s = Slot(g0, j, g0)
                        if s.any:
                            slot(s)

        block = ctx.enter_context(nc.Block())

        PIECE = 512
        pieces = []
        for src, hi, lo, width in ((w1t, w1h, w1l, KT * FF), (w2t, w2h, w2l, FB * C)):
            fl = [t[:, :, :].rearrange("p a b -> p (a b)") for t in (hi, lo)]
            for c in range(0, width, PIECE):
                pieces.append((src[:, c:c + PIECE], fl[0][:, c:c + PIECE], fl[1][:, c:c + PIECE]))

        @block.sync
        def _(sp):
            def await_(semaphore, value):
                sp.wait_ge(semaphore, value)
                sp.sem_inc(s_gate, 1)

            sp.dma_start(vecs[:, :], vec[:, :]).then_inc(s_const, 16)
            QW = HEADS * (P + PAIRS - 1)
            sp.dma_start(wq[:, :, :].rearrange("p a b -> p (a b)"), wqkv[:, 0:QW]).then_inc(s_const, 16)
            sp.dma_start(wk[:, :, :].rearrange("p a b -> p (a b)"), wqkv[:, QW:QW + HEADS * P]).then_inc(s_const, 16)
            sp.dma_start(wv[:, :, :].rearrange("p a b -> p (a b)"), wqkv[:, QW + HEADS * P:QW + 2 * HEADS * P]).then_inc(s_const, 16)
            for b in range(2):
                sp.dma_start(x_in[b][:, :, :], xa[b, :, 0]).then_inc(s_xa[b], 16)
            sp.dma_start(nbias[:, :, :, :].rearrange("p a b c -> p (a b c)"), bias[:, :]).then_inc(s_const, 16)
            sp.dma_start(ident[:, :], ident_in[:, :]).then_inc(s_const, 16)
            sp.dma_start(wp[:, :, :].rearrange("p a b -> p (a b)"), wpt[:, :]).then_inc(s_const, 16)

            def residual(c_set, cj, kind, st):
                n = 2 * c_set - FIRST[kind] + cj // PAIRS
                sp.dma_start(y[cj % 2][:, 0:KT * tokens(kind)], xrs[kind][n, cj % PAIRS]).then_inc(s_xr[cj % 2], 16)

            def slot(s):
                g, j, t = s.set, s.j, s.t
                if s.st == TURNS - 1:
                    await_(s_split, len(pieces))
                    residual(0, 0, 0, 0)
                    residual(0, 1, 0, 0)
                if s.ln2:
                    await_(v_l2, s.c2 * 10 + 10)
                    cs, cj = (g - 2, (j - 2) % TURNS) if j < 2 else (g - 1, j - 2)
                    T = tokens(s.kind2)
                    sp.dma_start(outs[s.kind2][2 * cs - FIRST[s.kind2] + cj // PAIRS, cj % PAIRS], r[:, 0:KT * T]).then_inc(s_out, 16)
                if s.st + 2 < LAST:
                    await_(p_v, t * 2 + 2)
                    j2 = (j + 2) % TURNS
                    sp.dma_start(x_in[j % 2][:, :, :], xa[2 * (g + (j + 2) // TURNS) + j2 % 2, :, j2 // 2]).then_inc(s_xa[j % 2], 16)
                if s.front:
                    await_(v_qs, t * 2 + 2)
                    if s.st >= 2:
                        await_(p_s, t * 8 - 8)
                    for h in range(2):
                        for row, part in enumerate((q_hi, q_lo, q_hi, q_lo)):
                            a = 64 * h + KD * row
                            sp.dma_start(q_stack[j % 2][a:a + KD, :, :].bitcast(F32),
                                         part[64 * h:64 * h + 64, :].bitcast(F32)).then_inc(s_qst, 16)
                if s.ln1 and s.st + 2 < LAST + TURNS:
                    await_(v_l1, s.c1 * 10 + 8)
                    cs, cj = (g - 1, j + 2) if j + 2 < TURNS else (g, j + 2 - TURNS)
                    residual(cs, cj, KIND_OF[2 * ((s.st - 6) // TURNS)], s.st)
                if s.back:
                    await_(a_r, s.bt * 4 + 4)
                    i = s.bhead
                    for h in range(2):
                        sp.dma_start(relu_d[2 * s.bset + s.bj % 2, :, 64 * (i % 2):64 * (i % 2) + 64, i // 2, h, :]
                                     .rearrange("p d n -> d p n"), relu[64 * h:64 * h + 64, :, :]).then_inc(s_rf, 16)
                if TURNS - 1 <= s.st < LAST + TURNS - 1:
                    if s.back:
                        await_(s_rf, t * 32)
                    if s.ln1:
                        await_(p_proj, s.c1 * 2)
                    cs, cj = (g, 0) if j == TURNS - 1 else (g - 1, j + 1)
                    sp.dma_start(proj_in[cj % 2][:, :, :, :].rearrange("p a b n -> p (a b n)"),
                                 relu_d[2 * cs + cj // PAIRS, cj % PAIRS].rearrange("p a b n -> p (a b n)")).then_inc(s_pin[cj % 2], 16)

            run_slots(sp, slot)
            sp.wait_ge(s_out, 16 * GROUPS * PAIRS)

        @block.tensor
        def _(pe):
            pe.wait_ge(s_const, 16 * 7)
            pe.wait_ge(s_set, 4)

            def fc1(s, f):
                T = tokens(s.kindm)
                zh, zl = kt3(z_hi, T), kt3(z_lo, T)
                if f == 0:
                    pe.wait_ge(v_l1, s.cm * 10 + 10)
                if f >= 2:
                    pe.wait_ge(a_g, s.cm * 32 + 2 * (f - 2) + 2)
                elif s.st > TURNS + 1:
                    pe.wait_ge(a_g, s.cm * 32)
                n = 0
                for k in range(KT):
                    for w, x in ((w1h, zh), (w1h, zl), (w1l, zh)):
                        mm = pe.matmul(hid[f % 2][:, 0:T], w[:, k, f * P:(f + 1) * P], x[:, k, :],
                                       start=n == 0, stop=n == 3 * KT - 1)
                        n += 1
                mm.then_inc(p_h, 1)

            def fc2(s, f):
                T = tokens(s.kindm)
                if f == 0 and s.st > TURNS + 1:
                    pe.wait_ge(v_l2, (s.cm - 1) * 10 + 2)
                pe.wait_ge(g_hl, s.cm * 16 + f + 1)
                for c in range(KT):
                    for n, (w, x) in enumerate(((w2h, h_hi), (w2h, h_lo), (w2l, h_hi))):
                        mm = pe.matmul(acc[c][:, 0:T], w[:, f, c * P:(c + 1) * P], x[:, f % HRING, 0:T],
                                       start=f == 0 and n == 0, stop=f == FB - 1 and n == 2)
                mm.then_inc(p_c, 1)

            def stats(s, step, which):
                kind, c, steps, done = (s.kind1, s.c1, v_l1, p_l1) if which == 1 else (s.kind2, s.c2, v_l2, p_l2)
                T = tokens(kind)
                q = T // 4
                at = (1, 3, 5) if which == 1 else (3, 5, 7)
                pe.wait_ge(steps, c * 10 + at[step])
                if step == 0:
                    if which == 1 and s.ln2:
                        pe.wait_ge(v_l2, s.c2 * 10 + 8)
                    elif s.st >= 2 and s.st <= LAST + 1:
                        pe.wait_ge(a_pt, t_back_done(s))
                    mm = pe.matmul(tr[:, 0:T], mean_w[:, :], tsum[:, 0:T], start=True, stop=True)
                elif step == 1:
                    for j in range(4):
                        mm = pe.matmul(tr[0:q, j:j + 1], tsum[:, q * j:q * j + q], mean_w[:, 0:1], start=True, stop=True)
                else:
                    mm = pe.matmul(tr[:, 0:T], ones[0:q, :], rdiag[0:q, 0:T], start=True, stop=True)
                mm.then_inc(done, 1)

            def t_back_done(s):
                return s.t * 8 - 8

            def proj(s):
                rows, cols, _ = KINDS[s.kind1]
                T = tokens(s.kind1)
                pe.wait_ge(s_pin[s.j % 2], s.set * 64 + 16 * (s.j // 2 + 1) - 64)
                if s.front:
                    pe.wait_ge(a_v, s.t * 2 + 2)
                elif s.st <= LAST + 1:
                    pe.wait_ge(a_r, s.t * 4 - 4)
                if s.st > TURNS:
                    pe.wait_ge(v_y, s.c1 * 2)
                for c in range(KT):
                    for kk in range(KT):
                        x = proj_in[s.j % 2][:, kk, :, :].rearrange("p h (a b) -> p h a b", a=WR)[:, :, 0:rows, 0:cols]
                        mm = pe.matmul(mix[1 - c][:, 0:T], wp[:, kk, c * P:(c + 1) * P], x, start=kk == 0, stop=kk == KT - 1)
                    mm.then_inc(p_proj, 1)

            def slot(s):
                g, j, t = s.set, s.j, s.t
                i = s.head
                x = x_in[j % 2]

                def q_product():
                    pe.wait_ge(s_xa[j % 2], g * 64 + 16 * (j // 2 + 1))
                    if i > 0:
                        pe.wait_ge(v_f, g * 24 + 4 * (j - 2) + 4)
                    if s.st >= 2:
                        pe.wait_ge(a_r, t * 4 - 4)
                    elif s.st == 1:
                        pe.wait_ge(a_v, 2)
                    for p in range(PAIRS):
                        mm = pe.matmul(mix[0][:, 0:N], wq[:, i, PAIRS - 1 - p:PAIRS - 1 - p + P], x[:, p, :],
                                       start=p == 0, stop=p == PAIRS - 1)
                    mm.then_inc(p_q, 1)

                def k_product(n):
                    if n == 1:
                        pe.wait_ge(a_q, t + 1)
                    pe.matmul(mix[1 - n][:, 0:2 * N], wk[:, i, :], x[:, 2 * n:2 * n + 2, :].rearrange("p a b -> p (a b)"),
                              start=True, stop=True).then_inc(p_k, 1)

                def v_product(n):
                    pe.wait_ge(a_k, t * 2 + n + 1)
                    for p in range(2):
                        for m in range(2):
                            a = (2 * p + m) * P
                            mm = pe.matmul(mix[1 - n][0:HALF, a:a + P], x[:, 2 * n + p, HALF * m:HALF * (m + 1)], wv[:, i, :],
                                           start=True, stop=True)
                    mm.then_inc(p_v, 1)

                bt, bb = s.bt, (j - 1) % 2

                def scores(u):
                    p, h = u // 2, u % 2
                    if u == 0:
                        pe.wait_ge(s_qst, bt * 128 + 128)
                        pe.wait_ge(v_ks, bt * 2 + 2)
                    if u > 0 or s.st >= 2:
                        pe.wait_ge(v_s, bt * 8 + u)
                    a = 64 * h
                    k = k_stack[bb][a:a + 64, p // 2, N * (p % 2):N * (p % 2) + N]
                    for m in range(2):
                        mm = pe.matmul(sc[0:HALF, N * m:N * m + N], q_stack[bb][a:a + 64, p, HALF * m:HALF * m + HALF], k,
                                       start=True, stop=True)
                    mm.then_inc(p_s, 1)

                def transposes(u):
                    pe.wait_ge(v_p, bt * 8 + u + 1)
                    if u > 0 or s.st >= 2:
                        pe.wait_ge(a_pt, bt * 8 + u)
                    if u == 0 and s.ln1:
                        pe.wait_ge(v_l1, s.c1 * 10 + 6)
                    for m in range(2):
                        for n in range(2):
                            mm = pe.transpose(tr[0:HALF, N * m + HALF * n:N * m + HALF * (n + 1)],
                                              prob[u % 3][:, n, HALF * m:HALF * (m + 1)], ident[0:HALF, 0:HALF])
                    mm.then_inc(p_t, 1)

                def attend(u):
                    p, h = u // 2, u % 2
                    if u == 0:
                        pe.wait_ge(a_v, (t if s.front else bt) * 2 + 2)
                        if s.ln1:
                            pe.wait_ge(v_y, s.c1 * 2 + 2)
                    if h == 0 and p >= 2:
                        pe.wait_ge(a_r, bt * 4 + p - 1)
                    pe.wait_ge(a_pt, bt * 8 + u + 1)
                    for m in range(2):
                        mm = pe.matmul(mix[p % 2][64 * h:64 * h + 64, 0:N], vt[bb][:, p, m, 64 * h:64 * h + 64],
                                       probt[u % 2][:, m, :], start=m == 0, stop=m == 1)
                    mm.then_inc(p_o, 1)

                for f in range(FB):
                    if s.mlp:
                        if f >= HRING:
                            fc2(s, f - HRING)
                        fc1(s, f)
                    if s.front:
                        if f == Q_AT:
                            q_product()
                        if f in K_AT:
                            k_product(K_AT.index(f))
                        if f in V_AT:
                            v_product(V_AT.index(f))
                    if s.ln1 and f == PROJ_AT:
                        proj(s)
                    if s.ln2 and f in N2_AT:
                        stats(s, N2_AT.index(f), 2)
                    if s.ln1 and f in N1_AT:
                        stats(s, N1_AT.index(f), 1)
                done = EARLY
                for k in range(STEPS):
                    if s.back and k < UNITS:
                        scores(k)
                    if s.mlp:
                        for _ in range(FC2_AT.get(k, 0)):
                            fc2(s, done)
                            done += 1
                    if s.back and 0 <= k - 3 < UNITS:
                        transposes(k - 3)
                    if s.back and 0 <= k - 5 < UNITS:
                        attend(k - 5)

            run_slots(pe, slot)

        @block.scalar
        def _(act):
            act.wait_ge(s_const, 16 * 7)
            act.wait_ge(s_set, 4)

            def gelu(s, f):
                T = tokens(s.kindm)
                act.wait_ge(p_h, s.cm * 16 + f + 1)
                act.activation(h_hi[:, f % HRING, 0:T], hid[f % 2][:, 0:T], ACT.Gelu, bias=col("b1", f)).then_inc(a_g, 1)
                if s.st > TURNS + 1 or f >= 2:
                    act.wait_ge(g_hl, s.cm * 16 + f - 1)
                act.activation(h_f[f % 2][:, 0:T], hid[f % 2][:, 0:T], ACT.Gelu, bias=col("b1", f)).then_inc(a_g, 1)

            def square(s, which):
                kind, c, steps, src, done, at = ((s.kind1, s.c1, v_l1, y[s.j % 2], a_sq1, 2) if which == 1
                                                 else (s.kind2, s.c2, v_l2, r, a_sq2, 4))
                n = KT * tokens(kind)
                act.wait_ge(steps, c * 10 + at)
                act.activation(sq[:, 0:n], src[:, 0:n], ACT.Square).then_inc(done, 1)

            def slot(s):
                g, j, t, i = s.set, s.j, s.t, s.head
                for f in range(FB):
                    if s.mlp:
                        gelu(s, f)
                    if s.front:
                        if f == Q_AT:
                            act.wait_ge(p_q, t + 1)
                            if s.st >= 1:
                                act.wait_ge(v_conv, t * 26)
                            act.activation(qpad[:, 2:2 + WR, 2:2 + WR], win(mix[0][:, 0:N]), ACT.Identity,
                                           bias=col("bq", i)).then_inc(a_q, 1)
                        if f in K_AT:
                            n = K_AT.index(f)
                            act.wait_ge(p_k, t * 2 + n + 1)
                            if s.st >= 1 or n == 1:
                                act.wait_ge(v_ks, t * 2 + n)
                            act.activation(k_f[:, :], mix[1 - n][:, 0:2 * N], ACT.Identity, bias=col("bk", i)).then_inc(a_k, 1)
                        if f in V_AT:
                            n = V_AT.index(f)
                            act.wait_ge(p_v, t * 2 + n + 1)
                            act.activation(vt[j % 2][:, 2 * n:2 * n + 2, :, :].rearrange("p a b c -> p (a b c)"),
                                           mix[1 - n][0:HALF, :], ACT.Copy).then_inc(a_v, 1)
                    if s.ln2 and f == SQ2_AT:
                        square(s, 2)
                    if s.ln1 and f == SQ1_AT:
                        square(s, 1)
                bt, bi = s.bt, s.bhead
                for k in range(STEPS + 1):
                    u = k - 1
                    if s.back and 0 <= u < UNITS:
                        b = u % 2
                        act.wait_ge(v_s, bt * 8 + u + 1)
                        if u >= 3:
                            act.wait_ge(p_t, bt * 8 + u - 2)
                        elif s.st >= 2:
                            act.wait_ge(p_t, bt * 8)
                        for m in range(2):
                            e = act.activation(prob[u % 3][:, m, :], nscore[b][:, m, :], ACT.Exp, bias=nmax[b][:, m:m + 1],
                                               scale=-1.0, accum_out=psums[u % 3][:, m:m + 1])
                        e.then_inc(a_e, 1)
                    u = k - 3
                    if s.back and 0 <= u < UNITS:
                        act.wait_ge(p_t, bt * 8 + u + 1)
                        if u >= 2:
                            act.wait_ge(p_o, bt * 8 + u - 1)
                        act.activation(probt[u % 2][:, :, :].rearrange("p a b -> p (a b)"), tr[0:HALF, 0:2 * N],
                                       ACT.Copy).then_inc(a_pt, 1)
                    if s.back and k in (6, 8, 10, 12):
                        p = (k - 6) // 2
                        act.wait_ge(p_o, bt * 8 + 2 * p + 2)
                        if p == 0 and s.st >= 2:
                            act.wait_ge(s_rf, bt * 32)
                        if bi < HEADS - 1:
                            act.wait_ge(v_f, s.bset * 24 + 4 * s.bj + p + 1)
                        act.activation(relu[:, p, :], mix[p % 2][:, 0:N], ACT.Relu, bias=col("bv", bi)).then_inc(a_r, 1)

            run_slots(act, slot)

        @block.vector
        def _(dve):
            dve.wait_ge(s_const, 16 * 7)
            dve.memset(mean_w[:, :], 1.0 / C).then_inc(s_set, 1)
            dve.memset(ones[:, :], 1.0).then_inc(s_set, 1)
            dve.memset(qpad[:, :, :], 0.0).then_inc(s_set, 1)
            dve.memset(minus_half[:, :], -0.5).then_inc(s_set, 1)
            nb = nbias[:, :, :, :].rearrange("p a b c -> p (a b c)")
            dve.tensor_scalar(nb, nb, -1.0, None, ALU.mult).then_inc(s_setv, 1)
            a = VEC["dw"][0]
            dve.tensor_scalar(dws[:, 0:HEADS * TAPS], vecs[:, a:a + HEADS * TAPS], -SCALE, None, ALU.mult).then_inc(s_setv, 1)
            a = VEC["bdw"][0]
            dve.tensor_scalar(dws[:, HEADS * TAPS:], vecs[:, a:a + HEADS], -SCALE, None, ALU.mult).then_inc(s_setv, 1)
            dve.wait_ge(s_setv, 3)

            def norm(s, step, which):
                kind, c, sem_, stat, sqs, pw, src, base, names = (
                    (s.kind1, s.c1, v_l1, p_l1, a_sq1, g_p1, y[s.j % 2], 0, ("n1w", "n1b")) if which == 1
                    else (s.kind2, s.c2, v_l2, p_l2, a_sq2, g_p2, r, 2, ("n2w", "n2b")))
                T = tokens(kind)
                q = T // 4
                v = kt3(src, T)
                s3 = kt3(sq, T)
                if step > 0 or which == 2:
                    dve.wait_ge(sem_, c * 10 + base + step)
                if step == 0:
                    ins = dve.tensor_tensor(tsum[:, 0:T], v[:, 0, :], v[:, 1, :], ALU.add)
                elif step == 1:
                    dve.wait_ge(stat, c * 3 + 1)
                    ins = dve.tensor_tensor(v, v, tr[:, 0:T].unsqueeze(1).broadcast_to([P, KT, T]), ALU.subtract)
                elif step == 2:
                    dve.wait_ge(sqs, c + 1)
                    ins = dve.tensor_tensor(tsum[:, 0:T], s3[:, 0, :], s3[:, 1, :], ALU.add)
                elif step == 3:
                    dve.wait_ge(stat, c * 3 + 2)
                    ins = dve.tensor_scalar(vcol[0:q, :], tr[0:q, 0:4], EPS, None, ALU.add)
                elif step == 4:
                    dve.wait_ge(pw, c + 1)
                    ins = dve.tensor_tensor(rdiag[0:q, 0:T].rearrange("p (j n) -> p j n", j=4),
                                            ident[0:q, 0:q].unsqueeze(1).broadcast_to([q, 4, q]),
                                            rcol[0:q, :].unsqueeze(2).broadcast_to([q, 4, q]), ALU.mult)
                elif step == 5:
                    dve.wait_ge(stat, c * 3 + 3)
                    ins = dve.tensor_tensor(v, v, tr[:, 0:T].unsqueeze(1).broadcast_to([P, KT, T]), ALU.mult)
                else:
                    k = step - 6
                    dst = kt3(z[s.j % 2], T) if which == 1 else v
                    ins = dve.tensor_scalar(dst[:, k, :], v[:, k, :], col(names[0], k), col(names[1], k), ALU.mult, ALU.add)
                ins.then_inc(sem_, 1)

            def slot(s):
                g, j, t, i = s.set, s.j, s.t, s.head
                bt, bi = s.bt, s.bhead

                def read_sums():
                    T = tokens(s.kind2)
                    dve.wait_ge(p_c, s.c2 * 16 + 16)
                    if s.st > TURNS + 2:
                        dve.wait_ge(s_out, s.c2 * 16)
                    for c in range(KT):
                        dve.scalar_tensor_tensor(kt3(r, T)[:, c, :], acc[c][:, 0:T], col("b2", c), kt3(z[j % 2], T)[:, c, :],
                                                 ALU.add, ALU.add).then_inc(v_l2, 1)

                def conv_steps(a, b):
                    if a == 0:
                        dve.wait_ge(a_q, t + 1)
                        if s.st >= 1:
                            dve.wait_ge(v_qs, t * 2)
                    for k in range(a, b):
                        if k >= 2:
                            dve.wait_ge(v_conv, t * 26 + (k - 1 if k < TAPS else TAPS))
                        out = conv[k % 2][:, :]
                        if k == TAPS:
                            ins = dve.tensor_tensor(conv[0][:, :], conv[0][:, :], conv[1][:, :], ALU.add)
                        else:
                            x = qpad[:, k // 5:k // 5 + WR, k % 5:k % 5 + WR]
                            w = dws[:, i * TAPS + k:i * TAPS + k + 1]
                            if k == 0:
                                ins = dve.tensor_scalar(win(out), x, w, dws[:, HEADS * TAPS + i:HEADS * TAPS + i + 1],
                                                        ALU.mult, ALU.add)
                            elif k == 1:
                                ins = dve.tensor_scalar(win(out), x, w, None, ALU.mult)
                            else:
                                ins = dve.scalar_tensor_tensor(win(out), x, w, win(out), ALU.mult, ALU.add)
                        ins.then_inc(v_conv, 1)

                def k_split(n):
                    dve.wait_ge(a_k, t * 2 + n + 1)
                    if s.st >= 1 or n == 1:
                        dve.wait_ge(v_ks, t * 2 + n)
                    dve.tensor_copy(k_hi[:, :], k_f[:, :]).then_inc(v_kh, 1)
                    dve.wait_ge(v_kh, t * 2 + n + 1)
                    dve.scalar_tensor_tensor(k_stack[j % 2][:, n, :], k_hi[:, :].bitcast(F32), col("lo_rows"), k_f[:, :],
                                             ALU.mult, ALU.add).then_inc(v_ks, 1)

                def q_split():
                    dve.wait_ge(v_conv, t * 26 + 26)
                    if s.st >= 1:
                        dve.wait_ge(s_qst, t * 128)
                    dve.tensor_copy(q_hi[:, :], conv[0][:, :]).then_inc(v_qs, 1)
                    dve.wait_ge(v_qs, t * 2 + 1)
                    dve.tensor_tensor(q_lo[:, :], conv[0][:, :], q_hi[:, :].bitcast(F32), ALU.subtract).then_inc(v_qs, 1)

                def add_proj():
                    T = tokens(s.kind1)
                    dve.wait_ge(s_xr[j % 2], g * 64 + 16 * (j // 2 + 1) - 64)
                    for c in range(KT):
                        dve.wait_ge(p_proj, s.c1 * 2 + c + 1)
                        yc = kt3(y[j % 2], T)[:, c, :]
                        dve.scalar_tensor_tensor(yc, mix[1 - c][:, 0:T], col("bproj", c), yc, ALU.add, ALU.add).then_inc(v_y, 1)

                def scores_read(u):
                    b = u % 2
                    dve.wait_ge(p_s, bt * 8 + u + 1)
                    if u >= 2 or s.st >= 2:
                        dve.wait_ge(a_e, bt * 8 + u - 1)
                        dve.wait_ge(v_s, bt * 8 + u - 1)
                    dve.sem_inc(v_gate, 1)
                    for m in range(2):
                        ins = dve.tensor_tensor_reduce(nscore[b][:, m, :], sc[0:HALF, N * m:N * m + N], nbias[:, bi, m, :],
                                                       1.0, BIG, ALU.add, ALU.min, nmax[b][:, m:m + 1])
                    ins.then_inc(v_s, 1)

                def prob_scale(u):
                    dve.wait_ge(a_e, bt * 8 + u + 1)
                    dve.reciprocal(rsums[u % 3][:, :], psums[u % 3][:, :]).then_inc(v_rs, 1)
                    dve.wait_ge(v_rs, bt * 8 + u + 1)
                    for m in range(2):
                        ins = dve.tensor_scalar(prob[u % 3][:, m, :], prob[u % 3][:, m, :], rsums[u % 3][:, m:m + 1], None, ALU.mult)
                    ins.then_inc(v_p, 1)

                def next_feat(p):
                    b = (j - 1) % 2
                    dve.wait_ge(p_o, bt * 8 + 2 * p + 2)
                    if p == 0:
                        dve.wait_ge(s_xa[b], s.bset * 64 + 16 * (bi + 2))
                    dve.scalar_tensor_tensor(x_in[b][:, p, :], mix[p % 2][:, 0:N], col("bv", bi), x_in[b][:, p, :],
                                             ALU.add, ALU.add).then_inc(v_f, 1)

                def split_z(lo):
                    T = tokens(s.kind1)
                    n = KT * T
                    dve.wait_ge(v_l1, s.c1 * 10 + 8 + lo)
                    zz = z[j % 2]
                    if not lo:
                        if s.mlp:
                            dve.wait_ge(p_h, s.cm * 16 + 16)
                        dve.tensor_copy(z_hi[:, 0:n], zz[:, 0:n]).then_inc(v_l1, 1)
                    else:
                        dve.tensor_tensor(z_lo[:, 0:n], zz[:, 0:n], z_hi[:, 0:n].bitcast(F32), ALU.subtract).then_inc(v_l1, 1)

                norms = s.ln1 or s.ln2
                if s.ln2:
                    read_sums()
                    norm(s, 0, 2)
                if s.front:
                    conv_steps(0, 5 if norms else 3)
                s.ln2 and norm(s, 1, 2)
                s.front and k_split(0)
                s.ln2 and norm(s, 2, 2)
                if s.front:
                    conv_steps(*((5, 12) if norms else (3, 6)))
                    k_split(1)
                s.ln2 and norm(s, 3, 2)
                s.front and norms and conv_steps(12, 17)
                s.ln2 and norm(s, 4, 2)
                s.front and norms and conv_steps(17, 20)
                if s.ln1:
                    add_proj()
                    dve.wait_ge(v_y, s.c1 * 2 + 2)
                    norm(s, 0, 1)
                s.front and norms and conv_steps(20, 22)
                s.ln2 and norm(s, 5, 2)
                if s.front and norms:
                    conv_steps(22, 26)
                    q_split()
                s.ln1 and norm(s, 1, 1)
                if s.ln2:
                    norm(s, 6, 2)
                    norm(s, 7, 2)
                for step in (2, 3, 4, 5):
                    s.ln1 and norm(s, step, 1)
                for k in range(STEPS + 1):
                    if s.back and k < UNITS:
                        scores_read(k)
                    if s.front and not norms:
                        if k < 7:
                            conv_steps(6 + 3 * k, min(9 + 3 * k, 26))
                        elif k == 7:
                            q_split()
                    if s.back and 0 <= k - 2 < UNITS:
                        prob_scale(k - 2)
                    if s.ln1 and k < 4:
                        norm(s, 6 + k, 1) if k < 2 else split_z(k - 2)
                    if s.back and bi < HEADS - 1 and k in (6, 8, 10, 12):
                        next_feat((k - 6) // 2)

            run_slots(dve, slot)

        @block.gpsimd
        def _(pool):
            for n, (src, hi, lo) in enumerate(pieces + [(None, None, None)]):
                if n < len(pieces):
                    if n >= 2:
                        pool.wait_ge(s_split, n - 1)
                    pool.dma_start(y[n % 2][:, 0:PIECE], src).then_inc(s_stage[n % 2], 16)
                if n > 0:
                    _, hi, lo = pieces[n - 1]
                    src = y[(n - 1) % 2][:, 0:PIECE]
                    pool.wait_ge(s_stage[(n - 1) % 2], 16 * ((n - 1) // 2 + 1))
                    pool.tensor_copy(hi, src).then_inc(s_split_hi, 1)
                    pool.wait_ge(s_split_hi, n)
                    pool.tensor_tensor(lo, src, hi.bitcast(F32), ALU.subtract).then_inc(s_split, 1)
            pool.wait_ge(s_split, len(pieces))
            pool.wait_ge(s_set, 4)

            def rsqrt(s, which):
                kind, c, steps, done, at = ((s.kind1, s.c1, v_l1, g_p1, 4) if which == 1 else (s.kind2, s.c2, v_l2, g_p2, 6))
                q = tokens(kind) // 4
                pool.wait_ge(steps, c * 10 + at)
                pool.tensor_tensor(rcol[0:q, :], vcol[0:q, :], minus_half[0:q, :], ALU.pow).then_inc(done, 1)

            def slot(s):
                for f in range(FB):
                    if s.mlp:
                        T = tokens(s.kindm)
                        pool.wait_ge(a_g, s.cm * 32 + 2 * f + 2)
                        pool.tensor_tensor(h_lo[:, f % HRING, 0:T], h_f[f % 2][:, 0:T], h_hi[:, f % HRING, 0:T].bitcast(F32),
                                           ALU.subtract).then_inc(g_hl, 1)
                    if s.ln2 and f == N2_AT[1]:
                        rsqrt(s, 2)
                    if s.ln1 and f == N1_AT[1]:
                        rsqrt(s, 1)

            run_slots(pool, slot)


def _device(nc, in_shapes):
    aps = {n: nc.dram_tensor(f"in_{n}", s, F32, kind="ExternalInput").ap() for n, s in in_shapes.items()}
    relu_d = nc.dram_tensor("relu_d", (GROUPS, PAIRS, P, KT, 2, N), F32, kind="Internal").ap()
    outs = []
    for k, (rows, cols, n) in enumerate(KINDS):
        outs.append(nc.dram_tensor(f"out{k}", (n, PAIRS, P, KT * 2 * rows * cols), F32, kind="ExternalOutput").ap())
    build(nc, aps["xa"], relu_d, [aps[f"xr{k}"] for k in range(len(KINDS))], aps["wqkv"], aps["bias"], aps["w1t"], aps["w2t"],
          aps["wpt"], aps["vec"], aps["ident"], outs)


def kernel(x, L0_conv_Wqkv, L0_conv_bqkv, L0_conv_Wdw, L0_conv_bdw, L0_conv_Wproj, L0_conv_bproj, L0_conv_attn_bias,
           L0_conv_norm1_w, L0_conv_norm1_b, L0_conv_norm2_w, L0_conv_norm2_b, L0_conv_Wfc1, L0_conv_bfc1,
           L0_conv_Wfc2, L0_conv_bfc2):
    import concourse.bacc as _bacc
    from concourse.bass_utils import run_bass_kernel_spmd as _run

    x = np.ascontiguousarray(x)
    f32 = x.dtype
    pos, kind = positions()
    xp = np.zeros((IMAGES, C, NW * WR, NW * WR), f32)
    xp[:, :, :H, :W] = x
    arrays = {}
    xa = np.zeros((GROUPS, P, HEADS, PAIRS, N), f32)
    xrs = [np.zeros((n, PAIRS, P, KT, 2, rows, cols), f32) for rows, cols, n in KINDS]
    for g in range(GROUPS):
        (a, b), half = pos[g // 2], g % 2
        w = xp[8 * half:8 * half + 8, :, WR * a:WR * a + WR, WR * b:WR * b + WR].reshape(2, PAIRS, HEADS, D, N)
        xa[g] = w.transpose(0, 3, 2, 1, 4).reshape(P, HEADS, PAIRS, N)
        k = KIND_OF[g]
        rows, cols, _ = KINDS[k]
        w = xp[8 * half:8 * half + 8, :, WR * a:WR * a + rows, WR * b:WR * b + cols].reshape(2, PAIRS, KT, P, rows, cols)
        xrs[k][g - FIRST[k]] = w.transpose(1, 3, 2, 0, 4, 5)
    arrays["xa"] = xa
    for k, a in enumerate(xrs):
        arrays[f"xr{k}"] = a.reshape(a.shape[0], PAIRS, P, -1)

    wqkv = np.asarray(L0_conv_Wqkv)
    wq = np.zeros((2, D, HEADS, P + PAIRS - 1), f32)
    wk = np.zeros((2, D, HEADS, 2, 4, KD), f32)
    wv = np.zeros((2, D, HEADS, 2, D), f32)
    for h in range(2):
        for i in range(HEADS):
            a = 64 * h + PAIRS - 1
            wq[h, :, i, a:a + PAIRS * KD:PAIRS] = wqkv[i, 0:KD].T
            for c in range(4):
                wk[h, :, i, h, c] = wqkv[i, KD:2 * KD].T
            wv[h, :, i, h] = wqkv[i, 2 * KD:].T
    arrays["wqkv"] = np.concatenate([wq.reshape(P, -1), wk.reshape(P, -1), wv.reshape(P, -1)], 1)

    dist = np.abs(np.arange(WR)[:, None] - np.arange(WR)[None, :])
    idx = (dist[:, None, :, None] * WR + dist[None, :, None, :]).reshape(N, N)
    bias = np.asarray(L0_conv_attn_bias)[:, idx]
    arrays["bias"] = np.ascontiguousarray(bias.reshape(HEADS, 2, HALF, N).transpose(2, 0, 1, 3).reshape(HALF, -1))
    arrays["w1t"] = np.ascontiguousarray(np.asarray(L0_conv_Wfc1).T.reshape(KT, P, FF).transpose(1, 0, 2).reshape(P, -1))
    arrays["w2t"] = np.ascontiguousarray(np.asarray(L0_conv_Wfc2).T.reshape(FB, P, C).transpose(1, 0, 2).reshape(P, -1))
    arrays["wpt"] = np.ascontiguousarray(np.asarray(L0_conv_Wproj).T.reshape(KT, P, C).transpose(1, 0, 2).reshape(P, -1))

    bqkv = np.asarray(L0_conv_bqkv)
    rep = lambda a, n: np.tile(a.T, (n, 1))
    rep_q = lambda a: np.tile(np.repeat(a.T, PAIRS, 0), (2, 1))
    tile = lambda a, n: np.ascontiguousarray(np.asarray(a).reshape(n, P).T)
    lo_rows = np.zeros((2, 4, KD, 1), f32)
    lo_rows[:, 2:] = -1.0
    parts = {
        "bq": rep_q(bqkv[:, 0:KD]), "bk": rep(bqkv[:, KD:2 * KD], 8), "bv": rep(bqkv[:, 2 * KD:], 2),
        "bdw": rep_q(np.asarray(L0_conv_bdw)),
        "dw": rep_q(np.asarray(L0_conv_Wdw).reshape(HEADS, KD, TAPS).transpose(0, 2, 1).reshape(-1, KD)),
        "bproj": tile(L0_conv_bproj, KT), "n1w": tile(L0_conv_norm1_w, KT), "n1b": tile(L0_conv_norm1_b, KT),
        "n2w": tile(L0_conv_norm2_w, KT), "n2b": tile(L0_conv_norm2_b, KT), "b1": tile(L0_conv_bfc1, FB),
        "b2": tile(L0_conv_bfc2, KT), "lo_rows": lo_rows.reshape(P, 1),
    }
    arrays["vec"] = np.ascontiguousarray(np.concatenate([parts[n] for n in VEC], 1))
    arrays["ident"] = np.eye(P, dtype=f32)

    nc = _bacc.Bacc("TRN2", target_bir_lowering=False, num_devices=1)
    _device(nc, {n: a.shape for n, a in arrays.items()})
    res = _run(nc, [{f"in_{n}": a for n, a in arrays.items()}], core_ids=[0]).results[0]

    out = np.zeros((IMAGES, C, H, W), f32)
    for g in range(GROUPS):
        (a, b), half = pos[g // 2], g % 2
        k = KIND_OF[g]
        rows, cols, _ = KINDS[k]
        w = res[f"out{k}"][g - FIRST[k]].reshape(PAIRS, P, KT, 2, rows, cols).transpose(3, 0, 2, 1, 4, 5)
        out[8 * half:8 * half + 8, :, WR * a:WR * a + rows, WR * b:WR * b + cols] = w.reshape(8, C, rows, cols)
    return out
```

```python
from contextlib import ExitStack

import numpy as np
import concourse.bass as bass
from concourse import mybir

F32 = mybir.dt.float32
F32R = mybir.dt.float32r
ALU = mybir.AluOpType
ACT = mybir.ActivationFunctionType

IMAGES, C, H, W = 16, 256, 40, 40
WR = 14
N = WR * WR
HALF = N // 2
NW = -(-H // WR)
HEADS, KD, D = 4, 16, 64
FF = 2048
SCALE = KD ** -0.5
EPS = 1e-6
PAIRS = 4
P = 128
KT = C // P
FB = FF // P
PADW = WR + 4
TAPS = 25
HRING = 11
BIG = 3.0e38


def positions():
    pos = [(a, b) for a in range(NW) for b in range(NW)]
    kind = lambda ab: (min(WR, H - WR * ab[0]), min(WR, W - WR * ab[1]))
    return sorted(pos, key=lambda ab: (-kind(ab)[0] * kind(ab)[1], -kind(ab)[0])), kind


def kinds():
    pos, kind = positions()
    out = []
    for ab in pos:
        k = kind(ab)
        if out and out[-1][:2] == k:
            out[-1] = (*k, out[-1][2] + 2)
        else:
            out.append((*k, 2))
    return out


KINDS = kinds()
GROUPS = sum(k[2] for k in KINDS)
FIRST = [sum(k[2] for k in KINDS[:j]) for j in range(len(KINDS))]
KIND_OF = [j for j, k in enumerate(KINDS) for _ in range(k[2])]

VEC = {}
for _name, _n in (("bq", HEADS), ("bk", HEADS), ("bv", HEADS), ("bdw", HEADS), ("dw", HEADS * TAPS), ("bproj", KT),
                  ("n1w", KT), ("n1b", KT), ("n2w", KT), ("n2b", KT), ("b1", FB), ("b2", KT), ("lo_rows", 1)):
    VEC[_name] = (sum(n for _, n in VEC.values()), _n)
NVEC = sum(n for _, n in VEC.values())

EARLY = FB - HRING
STEPS = 13
UNITS = 2 * PAIRS
FEAT_AT = (7, 9, 11, 13)
TURNS = 2 * HEADS
SETS = GROUPS // 2
LAST = SETS * TURNS
Q_AT, K_AT, V_AT, PROJ_AT = 1, (2, 3), (4, 5), 7
N2_AT, N1_AT = (2, 5, 8), (12, 14, FB)
SQ2_AT, SQ1_AT = 3, 12
NORM1_END = {1: 8, 3: 9, 4: 10, 6: 11, 8: 12}


class Slot:

    def __init__(self, g, j, static):
        self.set, self.j = g, j
        self.t = g * TURNS + j
        t = self.st = static * TURNS + j
        self.front = t < LAST
        self.back = 1 <= t <= LAST
        self.ln1 = TURNS <= t < LAST + TURNS
        self.mlp = TURNS + 1 <= t < LAST + TURNS + 1
        self.ln2 = TURNS + 2 <= t < LAST + TURNS + 2
        self.ahead = 2 if self.front and self.back and not self.ln1 else 0
        self.any = self.front or self.back or self.ln1 or self.mlp or self.ln2
        kind = lambda on, c: KIND_OF[2 * (c // TURNS)] if on else None
        self.kind1, self.kindm, self.kind2 = kind(self.ln1, t - 8), kind(self.mlp, t - 9), kind(self.ln2, t - 10)
        self.c1, self.cm, self.c2 = self.t - 8, self.t - 9, self.t - 10
        self.head = j // 2
        self.bt = self.t - 1
        self.bj = (j - 1) % TURNS
        self.bhead = self.bj // 2
        self.bset = g if j else g - 1


def tokens(kind):
    return 2 * KINDS[kind][0] * KINDS[kind][1]


def program():
    total = SETS + 2
    kind = lambda g: KIND_OF[2 * g]
    same = lambda g: 2 <= g < SETS and kind(g - 2) == kind(g - 1) == kind(g)
    out, g = [], 0
    while g < total:
        e = g + 1
        while same(g) and same(e) and kind(e) == kind(g):
            e += 1
        out.append((g, e, e - g >= 2))
        g = e
    return out


def build(nc, xa, relu_d, xrs, wqkv, bias, w1t, w2t, wpt, vec, ident_in, outs):
    ctx = ExitStack()
    with ctx:
        def sb(name, shape, dt=F32):
            return ctx.enter_context(nc.sbuf_tensor(name, shape, dt))

        def sem(name):
            return ctx.enter_context(nc.semaphore(name))

        TM = 2 * N
        w1h, w1l = (sb(n, [P, KT, FF], F32R) for n in ("w1h", "w1l"))
        w2h, w2l = (sb(n, [P, FB, C], F32R) for n in ("w2h", "w2l"))
        wq = sb("wq", [P, HEADS, P + PAIRS - 1])
        wk = sb("wk", [P, HEADS, P])
        wv = sb("wv", [P, HEADS, P])
        wph, wpl = (sb(n, [P, KT, C], F32R) for n in ("wph", "wpl"))
        nbias = sb("nbias", [HALF, HEADS, 2, N])
        vecs = sb("vecs", [P, NVEC])
        ident = sb("ident", [HALF, HALF])
        small = sb("small", [P, 12])
        mean_f = small[:, 0:1]
        mean_w = sb("mean_w", [P, P], F32R)
        ones, minus_half = small[:, 4:8], small[:, 8:12]
        x_in = [sb(f"x_in{b}", [P, PAIRS, N]) for b in range(2)]
        qpad = sb("qpad", [P, PADW, PADW])
        conv = [sb(f"conv{b}", [P, N]) for b in range(2)]
        q_hi, q_lo = (sb(n, [P, N], F32R) for n in ("q_hi", "q_lo"))
        q_stack = [sb(f"q_stack{b}", [P, PAIRS, N], F32R) for b in range(2)]
        k_f = sb("k_f", [P, 2 * N])
        k_stack = [sb(f"k_stack{b}", [P, 2, 2 * N], F32R) for b in range(2)]
        vt = [sb(f"vt{b}", [HALF, PAIRS, 2, P]) for b in range(2)]
        nscore = [sb(f"nscore{b}", [HALF, 2, N]) for b in range(2)]
        nmax = [sb(f"nmax{b}", [HALF, 2]) for b in range(2)]
        prob = [sb(f"prob{b}", [HALF, 2, N]) for b in range(3)]
        psums = [sb(f"psums{b}", [HALF, 2]) for b in range(3)]
        rsums = [sb(f"rsums{b}", [HALF, 2]) for b in range(3)]
        probt = [sb(f"probt{b}", [HALF, 2, N]) for b in range(2)]
        relu = sb("relu", [P, PAIRS, N])
        proj_in = [sb(f"proj_in{b}", [P, KT, 2, N], F32R) for b in range(2)]
        proj_hi = sb("proj_hi", [P, KT, 2, N], F32R)
        y = [sb(f"y{b}", [P, KT * TM]) for b in range(2)]
        z = [sb(f"z{b}", [P, KT * TM]) for b in range(2)]
        z_hi, z_lo = (sb(n, [P, KT * TM], F32R) for n in ("z_hi", "z_lo"))
        h_f = [sb(f"h_f{b}", [P, TM]) for b in range(3)]
        h_hi = sb("h_hi", [P, HRING, TM], F32R)
        h_lo = sb("h_lo", [P, HRING, TM], F32R)
        r = sb("r", [P, KT * TM])
        tsum = sb("tsum", [P, TM])
        tsum_hi, tsum_lo = (sb(n, [P, TM], F32R) for n in ("tsum_hi", "tsum_lo"))
        sq = sb("sq", [P, KT * TM])
        vcol = sb("vcol", [HALF, 4])
        rcol = sb("rcol", [HALF, 4])
        rcol_hi, rcol_lo = (sb(n, [HALF, 4], F32R) for n in ("rcol_hi", "rcol_lo"))
        rdiag = [sb(f"rdiag_{n}", [HALF, TM], F32R) for n in ("hi", "lo")]
        hid = [ctx.enter_context(nc.psum_tensor(f"hid{b}", [P, 512], F32)) for b in range(2)]
        acc = [ctx.enter_context(nc.psum_tensor(f"acc{b}", [P, 512], F32)) for b in range(2)]
        mix = [ctx.enter_context(nc.psum_tensor(f"mix{b}", [P, 512], F32)) for b in range(2)]
        sc = ctx.enter_context(nc.psum_tensor("sc", [P, 512], F32))
        tr = ctx.enter_context(nc.psum_tensor("tr", [P, 512], F32))
        sc = [sc, hid[1]]

        s_const = sem("const_loaded")
        s_gate, v_gate = sem("sync_waited"), sem("vector_waited")
        s_stage = [sem(f"weights_staged{b}") for b in range(2)]
        s_split_hi = sem("weights_hi_done")
        s_split = sem("weights_split")
        s_set = sem("memsets_done")
        s_setv = sem("vector_consts_done")
        s_xa = [sem(f"x_loaded{b}") for b in range(2)]
        s_xr = [sem(f"residual_loaded{b}") for b in range(2)]
        s_pin = [sem(f"proj_input_loaded{b}") for b in range(2)]
        s_qst = sem("q_stacked")
        s_rf = sem("relu_stored")
        s_out = sem("out_stored")
        p_q, p_k, p_v = sem("q_product"), sem("k_product"), sem("v_product")
        p_s, p_t, p_o = sem("scores"), sem("transposed"), sem("attended")
        p_proj = sem("projected")
        p_h, p_c = sem("hidden"), sem("fc2_block")
        p_l1, p_l2 = sem("norm1_stats"), sem("norm2_stats")
        a_q, a_k, a_v = sem("q_copied"), sem("k_copied"), sem("v_copied")
        a_g = sem("gelu_done")
        a_e, a_pt, a_r = sem("exp_done"), sem("probt_copied"), sem("relu_done")
        a_sq1, a_sq2 = sem("norm1_squares"), sem("norm2_squares")
        v_s, v_rs, v_p = sem("scores_read"), sem("sums_inverted"), sem("prob_scaled")
        v_f = sem("feat_ready")
        v_conv = sem("conv_steps")
        v_qs = sem("q_split")
        v_kh, v_ks = sem("k_rounded"), sem("k_stacked")
        v_pj = sem("proj_input_split")
        v_y = sem("y_ready")
        v_l1, v_l2 = sem("norm1_steps"), sem("norm2_steps")
        g_hl = sem("h_lo_done")
        g_p1, g_p2 = sem("norm1_rsqrt"), sem("norm2_rsqrt")

        def col(name, j=0, rows=slice(0, P)):
            a = VEC[name][0] + j
            return vecs[rows, a:a + 1]

        def kt3(tile, T):
            return tile[:, 0:KT * T].rearrange("p (k n) -> p k n", k=KT)

        def win(ap):
            return ap.rearrange("p (a b) -> p a b", a=WR)

        def run_slots(eng, slot):
            for g0, g1, looped in program():
                if looped:
                    with eng.Fori(g0, g1) as g:
                        for j in range(TURNS):
                            slot(Slot(g, j, g0))
                else:
                    for j in range(TURNS):
                        s = Slot(g0, j, g0)
                        if s.any:
                            slot(s)

        block = ctx.enter_context(nc.Block())

        PIECE = 512
        pieces = []
        for src, hi, lo, width in ((w1t, w1h, w1l, KT * FF), (w2t, w2h, w2l, FB * C), (wpt, wph, wpl, KT * C)):
            fl = [t[:, :, :].rearrange("p a b -> p (a b)") for t in (hi, lo)]
            for c in range(0, width, PIECE):
                pieces.append((src[:, c:c + PIECE], fl[0][:, c:c + PIECE], fl[1][:, c:c + PIECE]))

        @block.sync
        def _(sp):
            def await_(semaphore, value):
                sp.wait_ge(semaphore, value)
                sp.sem_inc(s_gate, 1)

            sp.dma_start(vecs[:, :], vec[:, :]).then_inc(s_const, 16)
            QW = HEADS * (P + PAIRS - 1)
            sp.dma_start(wq[:, :, :].rearrange("p a b -> p (a b)"), wqkv[:, 0:QW]).then_inc(s_const, 16)
            sp.dma_start(wk[:, :, :].rearrange("p a b -> p (a b)"), wqkv[:, QW:QW + HEADS * P]).then_inc(s_const, 16)
            sp.dma_start(wv[:, :, :].rearrange("p a b -> p (a b)"), wqkv[:, QW + HEADS * P:QW + 2 * HEADS * P]).then_inc(s_const, 16)
            for b in range(2):
                sp.dma_start(x_in[b][:, :, :], xa[b, :, 0]).then_inc(s_xa[b], 16)
            sp.dma_start(nbias[:, :, :, :].rearrange("p a b c -> p (a b c)"), bias[:, :]).then_inc(s_const, 16)
            sp.dma_start(ident[:, :], ident_in[:, :]).then_inc(s_const, 16)

            def residual(c_set, cj, kind):
                n = 2 * c_set - FIRST[kind] + cj // PAIRS
                sp.dma_start(y[cj % 2][:, 0:KT * tokens(kind)], xrs[kind][n, cj % PAIRS]).then_inc(s_xr[cj % 2], 16)

            def slot(s):
                g, j, t = s.set, s.j, s.t
                if s.st == TURNS - 1:
                    await_(s_split, len(pieces))
                    residual(0, 0, 0)
                    residual(0, 1, 0)
                if s.ln2:
                    await_(v_l2, s.c2 * 13 + 13)
                    cs, cj = (g - 2, (j - 2) % TURNS) if j < 2 else (g - 1, j - 2)
                    T = tokens(s.kind2)
                    sp.dma_start(outs[s.kind2][2 * cs - FIRST[s.kind2] + cj // PAIRS, cj % PAIRS], r[:, 0:KT * T]).then_inc(s_out, 16)
                if s.st + 2 < LAST:
                    await_(p_v, t * 2 + 2)
                    j2 = (j + 2) % TURNS
                    sp.dma_start(x_in[j % 2][:, :, :], xa[2 * (g + (j + 2) // TURNS) + j2 % 2, :, j2 // 2]).then_inc(s_xa[j % 2], 16)
                if s.front:
                    await_(v_qs, t * 2 + 2)
                    if s.st >= 2:
                        await_(p_s, t * 8 - 8)
                    for h in range(2):
                        for row, part in enumerate((q_hi, q_lo, q_hi, q_lo)):
                            a = 64 * h + KD * row
                            sp.dma_start(q_stack[j % 2][a:a + KD, :, :].bitcast(F32),
                                         part[64 * h:64 * h + 64, :].bitcast(F32)).then_inc(s_qst, 16)
                if s.ln1 and s.st + 2 < LAST + TURNS:
                    await_(v_l1, s.c1 * 13 + 11)
                    cs, cj = (g - 1, j + 2) if j + 2 < TURNS else (g, j + 2 - TURNS)
                    residual(cs, cj, KIND_OF[2 * ((s.st - 6) // TURNS)])
                if s.back:
                    await_(a_r, s.bt * 4 + 4)
                    i = s.bhead
                    for h in range(2):
                        sp.dma_start(relu_d[2 * s.bset + s.bj % 2, :, 64 * (i % 2):64 * (i % 2) + 64, i // 2, h, :]
                                     .rearrange("p d n -> d p n"), relu[64 * h:64 * h + 64, :, :]).then_inc(s_rf, 16)
                if TURNS - 1 <= s.st < LAST + TURNS - 1:
                    if s.back:
                        await_(s_rf, t * 32)
                    if s.ln1:
                        await_(p_proj, s.c1 * 2)
                    cs, cj = (g, 0) if j == TURNS - 1 else (g - 1, j + 1)
                    sp.dma_start(proj_in[cj % 2][:, :, :, :].rearrange("p a b n -> p (a b n)").bitcast(F32),
                                 relu_d[2 * cs + cj // PAIRS, cj % PAIRS].rearrange("p a b n -> p (a b n)")).then_inc(s_pin[cj % 2], 16)

            run_slots(sp, slot)
            sp.wait_ge(s_out, 16 * GROUPS * PAIRS)

        @block.tensor
        def _(pe):
            pe.wait_ge(s_const, 16 * 6)
            pe.wait_ge(s_set, 5)

            def fc1(s, f):
                T = tokens(s.kindm)
                zh, zl = kt3(z_hi, T), kt3(z_lo, T)
                if f == 0:
                    pe.wait_ge(v_l1, s.cm * 13 + 13)
                if f >= 2:
                    pe.wait_ge(a_g, s.cm * 32 + 2 * (f - 2) + 2)
                elif s.st > TURNS + 1:
                    pe.wait_ge(a_g, s.cm * 32)
                if f == 1 and s.st <= LAST + 1:
                    pe.wait_ge(v_s, s.t * 8 - 8)
                n = 0
                for k in range(KT):
                    for w, x in ((w1h, zh), (w1h, zl), (w1l, zh)):
                        mm = pe.matmul(hid[f % 2][:, 0:T], w[:, k, f * P:(f + 1) * P], x[:, k, :],
                                       start=n == 0, stop=n == 3 * KT - 1)
                        n += 1
                mm.then_inc(p_h, 1)

            def fc2(s, f):
                T = tokens(s.kindm)
                if f == 0 and s.st > TURNS + 1:
                    pe.wait_ge(v_l2, (s.cm - 1) * 13 + 2)
                pe.wait_ge(g_hl, s.cm * 16 + f + 1)
                for c in range(KT):
                    for n, (w, x) in enumerate(((w2h, h_hi), (w2h, h_lo), (w2l, h_hi))):
                        mm = pe.matmul(acc[c][:, 0:T], w[:, f, c * P:(c + 1) * P], x[:, f % HRING, 0:T],
                                       start=f == 0 and n == 0, stop=f == FB - 1 and n == 2)
                mm.then_inc(p_c, 1)

            def stats(s, step, which):
                kind, c, steps, done = (s.kind1, s.c1, v_l1, p_l1) if which == 1 else (s.kind2, s.c2, v_l2, p_l2)
                T = tokens(kind)
                q = T // 4
                at = (3, 5, 8) if which == 1 else (5, 7, 10)
                pe.wait_ge(steps, c * 13 + at[step])
                if step == 0:
                    if which == 1 and s.ln2:
                        pe.wait_ge(v_l2, s.c2 * 13 + 11)
                    elif s.st >= 2 and s.st <= LAST + 1:
                        pe.wait_ge(a_pt, s.t * 8 - 8)
                    pe.matmul(tr[:, 0:T], mean_w[:, :], tsum_hi[:, 0:T], start=True, stop=False)
                    mm = pe.matmul(tr[:, 0:T], mean_w[:, :], tsum_lo[:, 0:T], start=False, stop=True)
                elif step == 1:
                    for j in range(4):
                        mm = pe.matmul(tr[0:q, j:j + 1], tsum[:, q * j:q * j + q], mean_f[:, 0:1], start=True, stop=True)
                else:
                    for n in range(2):
                        mm = pe.matmul(tr[:, 0:T], mean_w[0:q, :], rdiag[n][0:q, 0:T], start=n == 0, stop=n == 1)
                mm.then_inc(done, 1)

            def proj(s):
                rows, cols, _ = KINDS[s.kind1]
                T = tokens(s.kind1)
                pe.wait_ge(v_pj, s.c1 * 2 + 2)
                if s.front:
                    pe.wait_ge(a_v, s.t * 2 + 2)
                elif s.st <= LAST + 1:
                    pe.wait_ge(a_r, s.t * 4 - 4)
                if s.st > TURNS:
                    pe.wait_ge(v_y, s.c1 * 2)
                for c in range(KT):
                    n = 0
                    for kk in range(KT):
                        hi, lo = (x[:, kk, :, :].rearrange("p h (a b) -> p h a b", a=WR)[:, :, 0:rows, 0:cols]
                                  for x in (proj_hi, proj_in[s.j % 2]))
                        for w, x in ((wph, hi), (wph, lo), (wpl, hi)):
                            mm = pe.matmul(mix[1 - c][:, 0:T], w[:, kk, c * P:(c + 1) * P], x, start=n == 0, stop=n == 3 * KT - 1)
                            n += 1
                    mm.then_inc(p_proj, 1)

            def slot(s):
                g, j, t = s.set, s.j, s.t
                i = s.head
                x = x_in[j % 2]

                def q_product():
                    pe.wait_ge(s_xa[j % 2], g * 64 + 16 * (j // 2 + 1))
                    if i > 0:
                        pe.wait_ge(v_f, g * 24 + 4 * (j - 2) + 4)
                    if s.st >= 2:
                        pe.wait_ge(a_r, t * 4 - 4)
                    elif s.st == 1:
                        pe.wait_ge(a_v, 2)
                    for p in range(PAIRS):
                        mm = pe.matmul(mix[0][:, 0:N], wq[:, i, PAIRS - 1 - p:PAIRS - 1 - p + P], x[:, p, :],
                                       start=p == 0, stop=p == PAIRS - 1)
                    mm.then_inc(p_q, 1)

                def k_product(n):
                    if n == 1:
                        pe.wait_ge(a_q, t + 1)
                    pe.matmul(mix[1 - n][:, 0:2 * N], wk[:, i, :], x[:, 2 * n:2 * n + 2, :].rearrange("p a b -> p (a b)"),
                              start=True, stop=True).then_inc(p_k, 1)

                def v_product(n):
                    pe.wait_ge(a_k, t * 2 + n + 1)
                    for p in range(2):
                        for m in range(2):
                            a = (2 * p + m) * P
                            mm = pe.matmul(mix[1 - n][0:HALF, a:a + P], x[:, 2 * n + p, HALF * m:HALF * (m + 1)], wv[:, i, :],
                                           start=True, stop=True)
                    mm.then_inc(p_v, 1)

                bt, bb = s.bt, (j - 1) % 2

                def scores(u):
                    p, h = u // 2, u % 2
                    if u == 0:
                        pe.wait_ge(s_qst, bt * 128 + 128)
                        pe.wait_ge(v_ks, bt * 2 + 2)
                    if u >= 2 or s.st >= 2:
                        pe.wait_ge(v_s, bt * 8 + u - 1)
                    if u == 1 and s.mlp:
                        pe.wait_ge(a_g, s.cm * 32 + 32)
                    a = 64 * h
                    k = k_stack[bb][a:a + 64, p // 2, N * (p % 2):N * (p % 2) + N]
                    for m in range(2):
                        mm = pe.matmul(sc[u % 2][0:HALF, N * m:N * m + N], q_stack[bb][a:a + 64, p, HALF * m:HALF * m + HALF], k,
                                       start=True, stop=True)
                    mm.then_inc(p_s, 1)

                def transposes(u):
                    pe.wait_ge(v_p, bt * 8 + u + 1)
                    if u > 0 or s.st >= 2:
                        pe.wait_ge(a_pt, bt * 8 + u)
                    if u == 0 and s.ln1:
                        pe.wait_ge(v_l1, s.c1 * 13 + 9)
                    for m in range(2):
                        for n in range(2):
                            mm = pe.transpose(tr[0:HALF, N * m + HALF * n:N * m + HALF * (n + 1)],
                                              prob[u % 3][:, n, HALF * m:HALF * (m + 1)], ident[0:HALF, 0:HALF])
                    mm.then_inc(p_t, 1)

                def attend(u):
                    p, h = u // 2, u % 2
                    if u == 0:
                        pe.wait_ge(a_v, (t if s.front else bt) * 2 + 2)
                        if s.ln1:
                            pe.wait_ge(v_y, s.c1 * 2 + 2)
                    if h == 0 and p >= 2:
                        pe.wait_ge(a_r, bt * 4 + p - 1)
                    pe.wait_ge(a_pt, bt * 8 + u + 1)
                    for m in range(2):
                        mm = pe.matmul(mix[p % 2][64 * h:64 * h + 64, 0:N], vt[bb][:, p, m, 64 * h:64 * h + 64],
                                       probt[u % 2][:, m, :], start=m == 0, stop=m == 1)
                    mm.then_inc(p_o, 1)

                def step(k):
                    if s.back and k < UNITS:
                        scores(k)
                    if s.mlp and k < HRING:
                        fc2(s, EARLY + k)
                    if s.ln1 and FB + k in N1_AT:
                        stats(s, N1_AT.index(FB + k), 1)
                    if s.back and 0 <= k - 3 < UNITS:
                        transposes(k - 3)
                    if s.back and 0 <= k - 5 < UNITS:
                        attend(k - 5)

                for k in range(s.ahead):
                    step(k)
                for f in range(FB):
                    if s.mlp:
                        if f >= HRING:
                            fc2(s, f - HRING)
                        fc1(s, f)
                    if s.front:
                        if f == Q_AT:
                            q_product()
                        if f in K_AT:
                            k_product(K_AT.index(f))
                        if f in V_AT:
                            v_product(V_AT.index(f))
                    if s.ln1 and f == PROJ_AT:
                        proj(s)
                    if s.ln2 and f in N2_AT:
                        stats(s, N2_AT.index(f), 2)
                    if s.ln1 and f in N1_AT:
                        stats(s, N1_AT.index(f), 1)
                for k in range(s.ahead, STEPS):
                    step(k)

            run_slots(pe, slot)

        @block.scalar
        def _(act):
            act.wait_ge(s_const, 16 * 6)
            act.wait_ge(s_set, 5)

            def gelu(s, f):
                T = tokens(s.kindm)
                act.wait_ge(p_h, s.cm * 16 + f + 1)
                act.activation(h_hi[:, f % HRING, 0:T], hid[f % 2][:, 0:T], ACT.Gelu, bias=col("b1", f)).then_inc(a_g, 1)
                if s.st > TURNS + 1 or f >= 3:
                    act.wait_ge(g_hl, s.cm * 16 + max(f - 2, 0))
                act.activation(h_f[f % 3][:, 0:T], hid[f % 2][:, 0:T], ACT.Gelu, bias=col("b1", f)).then_inc(a_g, 1)

            def square(s, which):
                kind, c, steps, src, done, at = ((s.kind1, s.c1, v_l1, y[s.j % 2], a_sq1, 4) if which == 1
                                                 else (s.kind2, s.c2, v_l2, r, a_sq2, 6))
                n = KT * tokens(kind)
                act.wait_ge(steps, c * 13 + at)
                act.activation(sq[:, 0:n], src[:, 0:n], ACT.Square).then_inc(done, 1)

            def slot(s):
                g, j, t, i = s.set, s.j, s.t, s.head
                bt, bi = s.bt, s.bhead

                def step(k):
                    u = k - 1
                    if s.back and 0 <= u < UNITS:
                        b = u % 2
                        act.wait_ge(v_s, bt * 8 + u + 1)
                        if u >= 3:
                            act.wait_ge(p_t, bt * 8 + u - 2)
                        elif s.st >= 2:
                            act.wait_ge(p_t, bt * 8)
                        for m in range(2):
                            e = act.activation(prob[u % 3][:, m, :], nscore[b][:, m, :], ACT.Exp, bias=nmax[b][:, m:m + 1],
                                               scale=-1.0, accum_out=psums[u % 3][:, m:m + 1])
                        e.then_inc(a_e, 1)
                    u = k - 3
                    if s.back and 0 <= u < UNITS:
                        act.wait_ge(p_t, bt * 8 + u + 1)
                        if u >= 2:
                            act.wait_ge(p_o, bt * 8 + u - 1)
                        act.activation(probt[u % 2][:, :, :].rearrange("p a b -> p (a b)"), tr[0:HALF, 0:2 * N],
                                       ACT.Copy).then_inc(a_pt, 1)
                    if s.back and k in FEAT_AT:
                        p = FEAT_AT.index(k)
                        act.wait_ge(p_o, bt * 8 + 2 * p + 2)
                        if p == 0 and s.st >= 2:
                            act.wait_ge(s_rf, bt * 32)
                        if bi < HEADS - 1:
                            act.wait_ge(v_f, s.bset * 24 + 4 * s.bj + p + 1)
                        act.activation(relu[:, p, :], mix[p % 2][:, 0:N], ACT.Relu, bias=col("bv", bi)).then_inc(a_r, 1)

                for k in range(s.ahead):
                    step(k)
                for f in range(FB):
                    if s.mlp:
                        gelu(s, f)
                    if s.front:
                        if f == Q_AT:
                            act.wait_ge(p_q, t + 1)
                            if s.st >= 1:
                                act.wait_ge(v_conv, t * 26)
                            act.activation(qpad[:, 2:2 + WR, 2:2 + WR], win(mix[0][:, 0:N]), ACT.Identity,
                                           bias=col("bq", i)).then_inc(a_q, 1)
                        if f in K_AT:
                            n = K_AT.index(f)
                            act.wait_ge(p_k, t * 2 + n + 1)
                            if s.st >= 1 or n == 1:
                                act.wait_ge(v_ks, t * 2 + n)
                            act.activation(k_f[:, :], mix[1 - n][:, 0:2 * N], ACT.Identity, bias=col("bk", i)).then_inc(a_k, 1)
                        if f in V_AT:
                            n = V_AT.index(f)
                            act.wait_ge(p_v, t * 2 + n + 1)
                            act.activation(vt[j % 2][:, 2 * n:2 * n + 2, :, :].rearrange("p a b c -> p (a b c)"),
                                           mix[1 - n][0:HALF, :], ACT.Copy).then_inc(a_v, 1)
                    if s.ln2 and f == SQ2_AT:
                        square(s, 2)
                    if s.ln1 and f == SQ1_AT:
                        square(s, 1)
                for k in range(s.ahead, STEPS + 1):
                    step(k)

            run_slots(act, slot)

        @block.vector
        def _(dve):
            dve.wait_ge(s_const, 16 * 6)
            dve.memset(mean_f[:, :], 1.0 / C).then_inc(s_set, 1)
            dve.memset(ones[:, :], 1.0).then_inc(s_set, 1)
            dve.memset(qpad[:, :, :], 0.0).then_inc(s_set, 1)
            dve.memset(minus_half[:, :], -0.5).then_inc(s_set, 1)
            dve.wait_ge(s_set, 2)
            dve.tensor_copy(mean_w[:, :], mean_f[:, :].broadcast_to([P, P])).then_inc(s_set, 1)
            nb = nbias[:, :, :, :].rearrange("p a b c -> p (a b c)")
            dve.tensor_scalar(nb, nb, -1.0, None, ALU.mult).then_inc(s_setv, 1)
            a = VEC["bdw"][0]
            conv_cols = vecs[:, a:a + HEADS * (1 + TAPS)]
            dve.tensor_scalar(conv_cols, conv_cols, -SCALE, None, ALU.mult).then_inc(s_setv, 1)
            dve.wait_ge(s_setv, 2)

            def norm(s, step, which):
                kind, c, sem_, stat, sqs, pw, src, base, names = (
                    (s.kind1, s.c1, v_l1, p_l1, a_sq1, g_p1, y[s.j % 2], 0, ("n1w", "n1b")) if which == 1
                    else (s.kind2, s.c2, v_l2, p_l2, a_sq2, g_p2, r, 2, ("n2w", "n2b")))
                T = tokens(kind)
                q = T // 4
                v = kt3(src, T)
                s3 = kt3(sq, T)
                if step > 0 or which == 2:
                    dve.wait_ge(sem_, c * 13 + base + step)
                if step == 0:
                    ins = dve.tensor_tensor(tsum[:, 0:T], v[:, 0, :], v[:, 1, :], ALU.add)
                elif step == 1:
                    ins = dve.tensor_copy(tsum_hi[:, 0:T], tsum[:, 0:T])
                elif step == 2:
                    ins = dve.tensor_tensor(tsum_lo[:, 0:T], tsum[:, 0:T], tsum_hi[:, 0:T].bitcast(F32), ALU.subtract)
                elif step == 3:
                    dve.wait_ge(stat, c * 3 + 1)
                    ins = dve.tensor_tensor(v, v, tr[:, 0:T].unsqueeze(1).broadcast_to([P, KT, T]), ALU.subtract)
                elif step == 4:
                    dve.wait_ge(sqs, c + 1)
                    ins = dve.tensor_tensor(tsum[:, 0:T], s3[:, 0, :], s3[:, 1, :], ALU.add)
                elif step == 5:
                    dve.wait_ge(stat, c * 3 + 2)
                    ins = dve.tensor_scalar(vcol[0:q, :], tr[0:q, 0:4], EPS, 1.0 / C ** 2, ALU.add, ALU.mult)
                elif step in (6, 7):
                    dve.wait_ge(pw, c * 3 + step - 4)
                    part = (rcol_hi, rcol_lo)[step - 6]
                    ins = dve.tensor_tensor(rdiag[step - 6][0:q, 0:T].rearrange("p (j n) -> p j n", j=4),
                                            ident[0:q, 0:q].unsqueeze(1).broadcast_to([q, 4, q]),
                                            part[0:q, :].bitcast(F32).unsqueeze(2).broadcast_to([q, 4, q]), ALU.mult)
                elif step == 8:
                    dve.wait_ge(stat, c * 3 + 3)
                    ins = dve.tensor_tensor(v, v, tr[:, 0:T].unsqueeze(1).broadcast_to([P, KT, T]), ALU.mult)
                else:
                    k = step - 9
                    dst = kt3(z[s.j % 2], T) if which == 1 else v
                    ins = dve.tensor_scalar(dst[:, k, :], v[:, k, :], col(names[0], k), col(names[1], k), ALU.mult, ALU.add)
                ins.then_inc(sem_, 1)

            def slot(s):
                g, j, t, i = s.set, s.j, s.t, s.head
                bt, bi = s.bt, s.bhead

                def read_sums():
                    T = tokens(s.kind2)
                    dve.wait_ge(p_c, s.c2 * 16 + 16)
                    if s.st > TURNS + 2:
                        dve.wait_ge(s_out, s.c2 * 16)
                    for c in range(KT):
                        dve.scalar_tensor_tensor(kt3(r, T)[:, c, :], acc[c][:, 0:T], col("b2", c), kt3(z[j % 2], T)[:, c, :],
                                                 ALU.add, ALU.add).then_inc(v_l2, 1)

                def conv_steps(a, b):
                    if a == 0:
                        dve.wait_ge(a_q, t + 1)
                        if s.st >= 1:
                            dve.wait_ge(v_qs, t * 2)
                    for k in range(a, b):
                        if k >= 2:
                            dve.wait_ge(v_conv, t * 26 + (k - 1 if k < TAPS else TAPS))
                        out = conv[k % 2][:, :]
                        if k == TAPS:
                            ins = dve.tensor_tensor(conv[0][:, :], conv[0][:, :], conv[1][:, :], ALU.add)
                        else:
                            x = qpad[:, k // 5:k // 5 + WR, k % 5:k % 5 + WR]
                            w = col("dw", i * TAPS + k)
                            if k == 0:
                                ins = dve.tensor_scalar(win(out), x, w, col("bdw", i),
                                                        ALU.mult, ALU.add)
                            elif k == 1:
                                ins = dve.tensor_scalar(win(out), x, w, None, ALU.mult)
                            else:
                                ins = dve.scalar_tensor_tensor(win(out), x, w, win(out), ALU.mult, ALU.add)
                        ins.then_inc(v_conv, 1)

                def k_split(n):
                    dve.wait_ge(a_k, t * 2 + n + 1)
                    ks = k_stack[j % 2][:, n, :]
                    dve.tensor_copy(ks, k_f[:, :]).then_inc(v_kh, 1)
                    dve.wait_ge(v_kh, t * 2 + n + 1)
                    dve.scalar_tensor_tensor(ks, ks.bitcast(F32), col("lo_rows"), k_f[:, :], ALU.mult, ALU.add).then_inc(v_ks, 1)

                def q_split():
                    dve.wait_ge(v_conv, t * 26 + 26)
                    if s.st >= 1:
                        dve.wait_ge(s_qst, t * 128)
                    dve.tensor_copy(q_hi[:, :], conv[0][:, :]).then_inc(v_qs, 1)
                    dve.wait_ge(v_qs, t * 2 + 1)
                    dve.tensor_tensor(q_lo[:, :], conv[0][:, :], q_hi[:, :].bitcast(F32), ALU.subtract).then_inc(v_qs, 1)

                def proj_split():
                    x, hi = (a[:, :, :, :].rearrange("p a b n -> p (a b n)") for a in (proj_in[j % 2], proj_hi))
                    dve.wait_ge(s_pin[j % 2], g * 64 + 16 * (j // 2 + 1) - 64)
                    if s.st > TURNS:
                        dve.wait_ge(p_proj, s.c1 * 2)
                    dve.tensor_copy(hi, x.bitcast(F32)).then_inc(v_pj, 1)
                    dve.wait_ge(v_pj, s.c1 * 2 + 1)
                    dve.tensor_tensor(x, x.bitcast(F32), hi.bitcast(F32), ALU.subtract).then_inc(v_pj, 1)

                def add_proj():
                    T = tokens(s.kind1)
                    dve.wait_ge(s_xr[j % 2], g * 64 + 16 * (j // 2 + 1) - 64)
                    for c in range(KT):
                        dve.wait_ge(p_proj, s.c1 * 2 + c + 1)
                        yc = kt3(y[j % 2], T)[:, c, :]
                        dve.scalar_tensor_tensor(yc, mix[1 - c][:, 0:T], col("bproj", c), yc, ALU.add, ALU.add).then_inc(v_y, 1)

                def scores_read(u):
                    b = u % 2
                    dve.wait_ge(p_s, bt * 8 + u + 1)
                    if u >= 2 or s.st >= 2:
                        dve.wait_ge(a_e, bt * 8 + u - 1)
                        dve.wait_ge(v_s, bt * 8 + u - 1)
                    dve.sem_inc(v_gate, 1)
                    for m in range(2):
                        ins = dve.tensor_tensor_reduce(nscore[b][:, m, :], sc[b][0:HALF, N * m:N * m + N], nbias[:, bi, m, :],
                                                       1.0, BIG, ALU.add, ALU.min, nmax[b][:, m:m + 1])
                    ins.then_inc(v_s, 1)

                def prob_scale(u):
                    dve.wait_ge(a_e, bt * 8 + u + 1)
                    dve.reciprocal(rsums[u % 3][:, :], psums[u % 3][:, :]).then_inc(v_rs, 1)
                    dve.wait_ge(v_rs, bt * 8 + u + 1)
                    for m in range(2):
                        ins = dve.tensor_scalar(prob[u % 3][:, m, :], prob[u % 3][:, m, :], rsums[u % 3][:, m:m + 1], None, ALU.mult)
                    ins.then_inc(v_p, 1)

                def next_feat(p):
                    b = (j - 1) % 2
                    dve.wait_ge(p_o, bt * 8 + 2 * p + 2)
                    if p == 0:
                        dve.wait_ge(s_xa[b], s.bset * 64 + 16 * (bi + 2))
                    dve.scalar_tensor_tensor(x_in[b][:, p, :], mix[p % 2][:, 0:N], col("bv", bi), x_in[b][:, p, :],
                                             ALU.add, ALU.add).then_inc(v_f, 1)

                def split_z(lo):
                    T = tokens(s.kind1)
                    n = KT * T
                    dve.wait_ge(v_l1, s.c1 * 13 + 11 + lo)
                    zz = z[j % 2]
                    if not lo:
                        if s.mlp:
                            dve.wait_ge(p_h, s.cm * 16 + 16)
                        dve.tensor_copy(z_hi[:, 0:n], zz[:, 0:n]).then_inc(v_l1, 1)
                    else:
                        dve.tensor_tensor(z_lo[:, 0:n], zz[:, 0:n], z_hi[:, 0:n].bitcast(F32), ALU.subtract).then_inc(v_l1, 1)

                norms = s.ln1 or s.ln2

                def steps(which, *numbers):
                    for n in numbers:
                        norm(s, n, which)

                for k in range(s.ahead):
                    scores_read(k)
                if s.ln2:
                    read_sums()
                    steps(2, 0, 1, 2)
                if s.front:
                    conv_steps(0, 4)
                s.ln2 and steps(2, 3)
                s.front and k_split(0)
                s.ln2 and steps(2, 4)
                s.ln1 and proj_split()
                s.front and conv_steps(4, 7 if norms else 8)
                s.ln2 and steps(2, 5)
                s.front and norms and conv_steps(7, 9)
                s.ln2 and steps(2, 6, 7)
                s.front and k_split(1)
                s.front and norms and conv_steps(9, 16)
                if s.ln1:
                    add_proj()
                    dve.wait_ge(v_y, s.c1 * 2 + 2)
                    norm(s, 0, 1)
                s.ln1 and steps(1, 1, 2)
                s.ln2 and steps(2, 8)
                s.front and norms and conv_steps(16, 20)
                s.ln1 and steps(1, 3)
                s.front and norms and conv_steps(20, 24)
                s.ln1 and steps(1, 4)
                if s.front and norms:
                    conv_steps(24, 26)
                    q_split()
                s.ln1 and steps(1, 5)
                s.ln2 and steps(2, 9, 10)
                s.ln1 and steps(1, 6, 7)
                for k in range(s.ahead, STEPS + 1):
                    if s.back and k < UNITS:
                        scores_read(k)
                    if s.front and not norms:
                        if 2 <= k < 8:
                            conv_steps(2 + 3 * k, 5 + 3 * k)
                        elif k == 8:
                            q_split()
                    if s.back and 0 <= k - 2 < UNITS:
                        prob_scale(k - 2)
                    if s.ln1 and k in NORM1_END:
                        n = NORM1_END[k]
                        norm(s, n, 1) if n < 11 else split_z(n - 11)
                    if s.back and bi < HEADS - 1 and k in FEAT_AT:
                        next_feat(FEAT_AT.index(k))

            run_slots(dve, slot)

        @block.gpsimd
        def _(pool):
            for n, (src, hi, lo) in enumerate(pieces + [(None, None, None)]):
                if n < len(pieces):
                    if n >= 2:
                        pool.wait_ge(s_split, n - 1)
                    pool.dma_start(y[n % 2][:, 0:PIECE], src).then_inc(s_stage[n % 2], 16)
                if n > 0:
                    _, hi, lo = pieces[n - 1]
                    src = y[(n - 1) % 2][:, 0:PIECE]
                    pool.wait_ge(s_stage[(n - 1) % 2], 16 * ((n - 1) // 2 + 1))
                    pool.tensor_copy(hi, src).then_inc(s_split_hi, 1)
                    pool.wait_ge(s_split_hi, n)
                    pool.tensor_tensor(lo, src, hi.bitcast(F32), ALU.subtract).then_inc(s_split, 1)
            pool.wait_ge(s_split, len(pieces))
            pool.wait_ge(s_set, 5)

            def rsqrt(s, which):
                kind, c, steps, done, at = ((s.kind1, s.c1, v_l1, g_p1, 6) if which == 1 else (s.kind2, s.c2, v_l2, g_p2, 8))
                q = tokens(kind) // 4
                pool.wait_ge(steps, c * 13 + at)
                pool.tensor_tensor(rcol[0:q, :], vcol[0:q, :], minus_half[0:q, :], ALU.pow).then_inc(done, 1)
                pool.wait_ge(done, c * 3 + 1)
                pool.tensor_tensor(rcol_hi[0:q, :], rcol[0:q, :], ones[0:q, :], ALU.mult).then_inc(done, 1)
                pool.wait_ge(done, c * 3 + 2)
                pool.tensor_tensor(rcol_lo[0:q, :], rcol[0:q, :], rcol_hi[0:q, :].bitcast(F32), ALU.subtract).then_inc(done, 1)

            def slot(s):
                for f in range(FB):
                    if s.ln2 and f == N2_AT[1]:
                        rsqrt(s, 2)
                    if s.ln1 and f == N1_AT[1]:
                        rsqrt(s, 1)
                    if s.mlp:
                        T = tokens(s.kindm)
                        pool.wait_ge(a_g, s.cm * 32 + 2 * f + 2)
                        pool.tensor_tensor(h_lo[:, f % HRING, 0:T], h_f[f % 3][:, 0:T], h_hi[:, f % HRING, 0:T].bitcast(F32),
                                           ALU.subtract).then_inc(g_hl, 1)

            run_slots(pool, slot)


def _device(nc, in_shapes):
    aps = {n: nc.dram_tensor(f"in_{n}", s, F32, kind="ExternalInput").ap() for n, s in in_shapes.items()}
    relu_d = nc.dram_tensor("relu_d", (GROUPS, PAIRS, P, KT, 2, N), F32, kind="Internal").ap()
    outs = []
    for k, (rows, cols, n) in enumerate(KINDS):
        outs.append(nc.dram_tensor(f"out{k}", (n, PAIRS, P, KT * 2 * rows * cols), F32, kind="ExternalOutput").ap())
    build(nc, aps["xa"], relu_d, [aps[f"xr{k}"] for k in range(len(KINDS))], aps["wqkv"], aps["bias"], aps["w1t"], aps["w2t"],
          aps["wpt"], aps["vec"], aps["ident"], outs)


def kernel(x, L0_conv_Wqkv, L0_conv_bqkv, L0_conv_Wdw, L0_conv_bdw, L0_conv_Wproj, L0_conv_bproj, L0_conv_attn_bias,
           L0_conv_norm1_w, L0_conv_norm1_b, L0_conv_norm2_w, L0_conv_norm2_b, L0_conv_Wfc1, L0_conv_bfc1,
           L0_conv_Wfc2, L0_conv_bfc2):
    import concourse.bacc as _bacc
    from concourse.bass_utils import run_bass_kernel_spmd as _run

    x = np.ascontiguousarray(x)
    f32 = x.dtype
    pos, kind = positions()
    xp = np.zeros((IMAGES, C, NW * WR, NW * WR), f32)
    xp[:, :, :H, :W] = x
    arrays = {}
    xa = np.zeros((GROUPS, P, HEADS, PAIRS, N), f32)
    xrs = [np.zeros((n, PAIRS, P, KT, 2, rows, cols), f32) for rows, cols, n in KINDS]
    for g in range(GROUPS):
        (a, b), half = pos[g // 2], g % 2
        w = xp[8 * half:8 * half + 8, :, WR * a:WR * a + WR, WR * b:WR * b + WR].reshape(2, PAIRS, HEADS, D, N)
        xa[g] = w.transpose(0, 3, 2, 1, 4).reshape(P, HEADS, PAIRS, N)
        k = KIND_OF[g]
        rows, cols, _ = KINDS[k]
        w = xp[8 * half:8 * half + 8, :, WR * a:WR * a + rows, WR * b:WR * b + cols].reshape(2, PAIRS, KT, P, rows, cols)
        xrs[k][g - FIRST[k]] = w.transpose(1, 3, 2, 0, 4, 5)
    arrays["xa"] = xa
    for k, a in enumerate(xrs):
        arrays[f"xr{k}"] = a.reshape(a.shape[0], PAIRS, P, -1)

    wqkv = np.asarray(L0_conv_Wqkv)
    wq = np.zeros((2, D, HEADS, P + PAIRS - 1), f32)
    wk = np.zeros((2, D, HEADS, 2, 4, KD), f32)
    wv = np.zeros((2, D, HEADS, 2, D), f32)
    for h in range(2):
        for i in range(HEADS):
            a = 64 * h + PAIRS - 1
            wq[h, :, i, a:a + PAIRS * KD:PAIRS] = wqkv[i, 0:KD].T
            for c in range(4):
                wk[h, :, i, h, c] = wqkv[i, KD:2 * KD].T
            wv[h, :, i, h] = wqkv[i, 2 * KD:].T
    arrays["wqkv"] = np.concatenate([wq.reshape(P, -1), wk.reshape(P, -1), wv.reshape(P, -1)], 1)

    dist = np.abs(np.arange(WR)[:, None] - np.arange(WR)[None, :])
    idx = (dist[:, None, :, None] * WR + dist[None, :, None, :]).reshape(N, N)
    bias = np.asarray(L0_conv_attn_bias)[:, idx]
    arrays["bias"] = np.ascontiguousarray(bias.reshape(HEADS, 2, HALF, N).transpose(2, 0, 1, 3).reshape(HALF, -1))
    arrays["w1t"] = np.ascontiguousarray(np.asarray(L0_conv_Wfc1).T.reshape(KT, P, FF).transpose(1, 0, 2).reshape(P, -1))
    arrays["w2t"] = np.ascontiguousarray(np.asarray(L0_conv_Wfc2).T.reshape(FB, P, C).transpose(1, 0, 2).reshape(P, -1))
    arrays["wpt"] = np.ascontiguousarray(np.asarray(L0_conv_Wproj).T.reshape(KT, P, C).transpose(1, 0, 2).reshape(P, -1))

    bqkv = np.asarray(L0_conv_bqkv)
    rep = lambda a, n: np.tile(a.T, (n, 1))
    rep_q = lambda a: np.tile(np.repeat(a.T, PAIRS, 0), (2, 1))
    tile = lambda a, n: np.ascontiguousarray(np.asarray(a).reshape(n, P).T)
    lo_rows = np.zeros((2, 4, KD, 1), f32)
    lo_rows[:, 2:] = -1.0
    parts = {
        "bq": rep_q(bqkv[:, 0:KD]), "bk": rep(bqkv[:, KD:2 * KD], 8), "bv": rep(bqkv[:, 2 * KD:], 2),
        "bdw": rep_q(np.asarray(L0_conv_bdw)),
        "dw": rep_q(np.asarray(L0_conv_Wdw).reshape(HEADS, KD, TAPS).transpose(0, 2, 1).reshape(-1, KD)),
        "bproj": tile(L0_conv_bproj, KT), "n1w": tile(L0_conv_norm1_w, KT), "n1b": tile(L0_conv_norm1_b, KT),
        "n2w": tile(L0_conv_norm2_w, KT), "n2b": tile(L0_conv_norm2_b, KT), "b1": tile(L0_conv_bfc1, FB),
        "b2": tile(L0_conv_bfc2, KT), "lo_rows": lo_rows.reshape(P, 1),
    }
    arrays["vec"] = np.ascontiguousarray(np.concatenate([parts[n] for n in VEC], 1))
    arrays["ident"] = np.eye(HALF, dtype=f32)

    nc = _bacc.Bacc("TRN2", target_bir_lowering=False, num_devices=1)
    _device(nc, {n: a.shape for n, a in arrays.items()})
    res = _run(nc, [{f"in_{n}": a for n, a in arrays.items()}], core_ids=[0]).results[0]

    out = np.zeros((IMAGES, C, H, W), f32)
    for g in range(GROUPS):
        (a, b), half = pos[g // 2], g % 2
        k = KIND_OF[g]
        rows, cols, _ = KINDS[k]
        w = res[f"out{k}"][g - FIRST[k]].reshape(PAIRS, P, KT, 2, rows, cols).transpose(3, 0, 2, 1, 4, 5)
        out[8 * half:8 * half + 8, :, WR * a:WR * a + rows, WR * b:WR * b + cols] = w.reshape(8, C, rows, cols)
    return out
```
